# Optimizing a Trainium2 kernel written in Bass

```python
import numpy as np
import jax
import jax.numpy as jnp

def _softmax(x, axis=-1):
    return jax.nn.softmax(x, axis=axis)

def _gelu(x):
    return jax.nn.gelu(x, approximate=True)

def _silu(x):
    return jax.nn.silu(x)

def _sigmoid(x):
    return jax.nn.sigmoid(x)

def _layernorm(x, axis=-1, eps=1e-05):
    m = jnp.mean(x, axis=axis, keepdims=True)
    v = jnp.var(x, axis=axis, keepdims=True)
    return (x - m) / jnp.sqrt(v + eps)

def _scatter_add(tgt, idx, src, axis=0):
    return tgt.at[idx].add(src)

def _segment_sum(src, seg, n):
    return jax.ops.segment_sum(src, seg, n)
kernel_name = 'mk_xattn_seq_d1_seqx_r2_ce3723'

def setup_inputs(seed: int=0):
    np.random.seed(seed)
    _w = jnp.asarray

    def _rec_inputs():
        import jax
        import jax.numpy as jnp
        _rk = jax.random.key(seed)
        x = -0.000296 + 1 * jax.random.normal(jax.random.fold_in(_rk, 1), (2, 2048, 640), jnp.float32)
        _lenS = 2048 - jax.random.randint(jax.random.fold_in(_rk, 7), (2,), 0, max(1, 2048 // 4) + 1, jnp.int32)
        _lenS2 = 154 - jax.random.randint(jax.random.fold_in(_rk, 8), (2,), 0, max(1, 154 // 4) + 1, jnp.int32)
        _ctx_2048P = jax.random.normal(jax.random.fold_in(_rk, 11), (2, 16, 1024), jnp.float32)
        _ctx_2048c = jax.random.dirichlet(jax.random.fold_in(_rk, 511), 0.3 * jnp.ones((16,), jnp.float32), (2, 154))
        _ctx_2048t = jnp.einsum('bsk,bkd->bsd', _ctx_2048c, _ctx_2048P)
        _ctx_2048t = _ctx_2048t * jax.lax.rsqrt(jnp.mean(jnp.square(_ctx_2048t)) + 1e-12) * 0.953939
        ctx_2048 = 0.00118529 + 0.99962 * (_ctx_2048t + 0.3 * jax.random.normal(jax.random.fold_in(_rk, 611), (2, 154, 1024), jnp.float32))
        fside_Bx4x4_0 = jax.random.uniform(jax.random.fold_in(_rk, 12), (2, 4, 4), jnp.float32, 0.0, 0.981965)
        return (x, ctx_2048, fside_Bx4x4_0)
    x, ctx_2048, fside_Bx4x4_0 = _rec_inputs()

    def _L0_xattn_setup():
        import jax, jax.numpy as jnp
        import numpy as np
        HEADS = 20
        NUM_IP_TOKENS = 4
        NUM_DUMMY_TOKENS = 4
        IP_SCALE = 1.0
        ASPECT_RATIO = 1.0
        NEG = -10000.0

        def _grid_hw(seq_len, aspect_ratio):
            width = int((seq_len / aspect_ratio) ** 0.5)
            height = seq_len // width
            while width * height != seq_len:
                if width * height < seq_len:
                    width += 1
                else:
                    width -= 1
                height = seq_len // width
            return (height, width)

        def _sdpa(q, k, v, mask=None):
            dh = q.shape[-1]
            scores = jnp.einsum('bhqd,bhkd->bhqk', q, k) / jnp.sqrt(jnp.asarray(dh, q.dtype))
            if mask is not None:
                scores = scores + mask
            probs = jax.nn.softmax(scores, axis=-1)
            return jnp.einsum('bhqk,bhkd->bhqd', probs, v)

        def _split_heads(x, heads):
            b, l, d = x.shape
            return x.reshape(b, l, heads, d // heads).transpose(0, 2, 1, 3)

        def _merge_heads(x):
            b, h, l, dh = x.shape
            return x.transpose(0, 2, 1, 3).reshape(b, l, h * dh)

        def _ip_mask(bbox, batch_size, seq_len, dtype):
            M = bbox.shape[1]
            height, width = _grid_hw(seq_len, ASPECT_RATIO)
            x = jnp.linspace(0.0, 1.0, width, dtype=dtype)
            y = jnp.linspace(0.0, 1.0, height, dtype=dtype)
            yg, xg = jnp.meshgrid(y, x, indexing='ij')
            xg = xg.reshape(-1)
            yg = yg.reshape(-1)
            x1, y1, x2, y2 = (bbox[..., 0:1], bbox[..., 1:2], bbox[..., 2:3], bbox[..., 3:4])
            inside = (xg >= x1) & (xg <= x2) & (yg >= y1) & (yg <= y2)
            ip_mask = jnp.where(inside, 0.0, NEG).astype(dtype)
            ip_mask = jnp.transpose(ip_mask, (0, 2, 1))[:, None]
            ip_mask = jnp.repeat(ip_mask, NUM_IP_TOKENS // M, axis=-1)
            dummy = jnp.where(jnp.any(inside, axis=1), NEG, 0.0).astype(dtype)
            dummy = jnp.repeat(dummy[:, None, :, None], NUM_DUMMY_TOKENS, axis=-1)
            return jnp.concatenate([dummy, ip_mask], axis=-1)
        key = jax.random.key(seed)
        ks = jax.random.split(key, 12)
        B, S, D, C = (4, 2048, 640, 1024)
        text_len, M = (77, 4)
        hidden_states = jax.random.normal(ks[0], (B, S, D), jnp.float32)
        encoder_hidden_states = jax.random.normal(ks[1], (B, text_len + NUM_IP_TOKENS + NUM_DUMMY_TOKENS, C), jnp.float32)
        p1 = jax.random.uniform(ks[2], (B, M, 2), jnp.float32)
        p2 = jax.random.uniform(ks[3], (B, M, 2), jnp.float32)
        bbox = jnp.concatenate([jnp.minimum(p1, p2), jnp.maximum(p1, p2)], axis=-1)
        s = 0.02
        w_q = jax.random.normal(ks[4], (D, D), jnp.float32) * s
        w_k = jax.random.normal(ks[5], (C, D), jnp.float32) * s
        w_v = jax.random.normal(ks[6], (C, D), jnp.float32) * s
        w_k_ip = jax.random.normal(ks[7], (C, D), jnp.float32) * s
        w_v_ip = jax.random.normal(ks[8], (C, D), jnp.float32) * s
        w_out = jax.random.normal(ks[9], (D, D), jnp.float32) * s
        b_out = jnp.zeros((D,), jnp.float32)
        return {'hidden_states': hidden_states, 'encoder_hidden_states': encoder_hidden_states, 'bbox': bbox, 'w_q': w_q, 'w_k': w_k, 'w_v': w_v, 'w_k_ip': w_k_ip, 'w_v_ip': w_v_ip, 'w_out': w_out, 'b_out': b_out}
    _L0_xattn_all = _L0_xattn_setup()
    _L0_xattn_in = {k: v for k, v in _L0_xattn_all.items() if k in ('w_q', 'w_k', 'w_v', 'w_k_ip', 'w_v_ip', 'w_out', 'b_out')}
    del _L0_xattn_all
    return {'x': x, 'ctx_2048': ctx_2048, 'fside_Bx4x4_0': fside_Bx4x4_0, 'L0_xattn_w_q': _L0_xattn_in['w_q'], 'L0_xattn_w_k': _L0_xattn_in['w_k'], 'L0_xattn_w_v': _L0_xattn_in['w_v'], 'L0_xattn_w_k_ip': _L0_xattn_in['w_k_ip'], 'L0_xattn_w_v_ip': _L0_xattn_in['w_v_ip'], 'L0_xattn_w_out': _L0_xattn_in['w_out'], 'L0_xattn_b_out': _L0_xattn_in['b_out']}

def reference(x, ctx_2048, fside_Bx4x4_0, L0_xattn_w_q, L0_xattn_w_k, L0_xattn_w_v, L0_xattn_w_k_ip, L0_xattn_w_v_ip, L0_xattn_w_out, L0_xattn_b_out):
    import jax
    import jax.numpy as jnp

    def _L0_xattn_ref(hidden_states, encoder_hidden_states, bbox, w_q, w_k, w_v, w_k_ip, w_v_ip, w_out, b_out):
        import jax, jax.numpy as jnp
        import numpy as np
        HEADS = 20
        NUM_IP_TOKENS = 4
        NUM_DUMMY_TOKENS = 4
        IP_SCALE = 1.0
        ASPECT_RATIO = 1.0
        NEG = -10000.0

        def _grid_hw(seq_len, aspect_ratio):
            width = int((seq_len / aspect_ratio) ** 0.5)
            height = seq_len // width
            while width * height != seq_len:
                if width * height < seq_len:
                    width += 1
                else:
                    width -= 1
                height = seq_len // width
            return (height, width)

        def _sdpa(q, k, v, mask=None):
            dh = q.shape[-1]
            scores = jnp.einsum('bhqd,bhkd->bhqk', q, k) / jnp.sqrt(jnp.asarray(dh, q.dtype))
            if mask is not None:
                scores = scores + mask
            probs = jax.nn.softmax(scores, axis=-1)
            return jnp.einsum('bhqk,bhkd->bhqd', probs, v)

        def _split_heads(x, heads):
            b, l, d = x.shape
            return x.reshape(b, l, heads, d // heads).transpose(0, 2, 1, 3)

        def _merge_heads(x):
            b, h, l, dh = x.shape
            return x.transpose(0, 2, 1, 3).reshape(b, l, h * dh)

        def _ip_mask(bbox, batch_size, seq_len, dtype):
            M = bbox.shape[1]
            height, width = _grid_hw(seq_len, ASPECT_RATIO)
            x = jnp.linspace(0.0, 1.0, width, dtype=dtype)
            y = jnp.linspace(0.0, 1.0, height, dtype=dtype)
            yg, xg = jnp.meshgrid(y, x, indexing='ij')
            xg = xg.reshape(-1)
            yg = yg.reshape(-1)
            x1, y1, x2, y2 = (bbox[..., 0:1], bbox[..., 1:2], bbox[..., 2:3], bbox[..., 3:4])
            inside = (xg >= x1) & (xg <= x2) & (yg >= y1) & (yg <= y2)
            ip_mask = jnp.where(inside, 0.0, NEG).astype(dtype)
            ip_mask = jnp.transpose(ip_mask, (0, 2, 1))[:, None]
            ip_mask = jnp.repeat(ip_mask, NUM_IP_TOKENS // M, axis=-1)
            dummy = jnp.where(jnp.any(inside, axis=1), NEG, 0.0).astype(dtype)
            dummy = jnp.repeat(dummy[:, None, :, None], NUM_DUMMY_TOKENS, axis=-1)
            return jnp.concatenate([dummy, ip_mask], axis=-1)
        B, S, D = hidden_states.shape
        residual = hidden_states
        end_pos = encoder_hidden_states.shape[1] - (NUM_IP_TOKENS + NUM_DUMMY_TOKENS)
        text = encoder_hidden_states[:, :end_pos]
        ip_h = encoder_hidden_states[:, end_pos:]
        q = _split_heads(hidden_states @ w_q, HEADS)
        k = _split_heads(text @ w_k, HEADS)
        v = _split_heads(text @ w_v, HEADS)
        out_text = _sdpa(q, k, v)
        out_text = _merge_heads(out_text)
        mask_ip = _ip_mask(bbox, B, S, hidden_states.dtype)
        k_ip = _split_heads(ip_h @ w_k_ip, HEADS)
        v_ip = _split_heads(ip_h @ w_v_ip, HEADS)
        out_ip = _merge_heads(_sdpa(q, k_ip, v_ip, mask=mask_ip))
        out = out_text + IP_SCALE * out_ip
        out = out @ w_out + b_out
        out = out + residual
        return out
    x = _L0_xattn_ref(x, ctx_2048, fside_Bx4x4_0, L0_xattn_w_q, L0_xattn_w_k, L0_xattn_w_v, L0_xattn_w_k_ip, L0_xattn_w_v_ip, L0_xattn_w_out, L0_xattn_b_out)
    return x

_drawn_inputs = setup_inputs


def setup_inputs(seed=0):
    import zlib

    import numpy as np

    out = dict(_drawn_inputs(seed))
    spreads = {'L0_xattn_b_out': (0.0, 0.1)}
    factors = {'L0_xattn_w_k': 3.015}
    for name, (base, spread) in spreads.items():
        noise = np.random.default_rng([zlib.crc32(name.encode()), seed]).standard_normal(out[name].shape)
        drawn = base * np.exp(spread * noise) if base else spread * noise
        out[name] = jnp.asarray(drawn.astype(out[name].dtype))
    for name, factor in factors.items():
        out[name] = (out[name] * factor).astype(out[name].dtype)
    return out
```

```python
from contextlib import ExitStack

import numpy as np

import concourse.bass as bass
from concourse import mybir

F32 = mybir.dt.float32
F32R = mybir.dt.float32r
BF16 = mybir.dt.bfloat16
ALU = mybir.AluOpType
ACT = mybir.ActivationFunctionType
AX_X = mybir.AxisListType.X

P = 128
BATCHES, SEQ, D = 2, 2048, 640
CTX, CTX_D = 154, 1024
HEADS, DH = 20, 32
IP = 8
DUMMIES = 4
TEXT = CTX - IP
REM = TEXT - P
TAIL = REM + IP
NEG = -10000.0
SCALE = float(np.float32(1.0) / np.sqrt(np.float32(DH)))

KC = D // P
CC = CTX_D // P
GROUPS = HEADS // 4
QB = 256
QT = QB // P
BLOCKS = BATCHES * SEQ // QB
PER_BATCH = BLOCKS // BATCHES
VW = DH + 1
HALF = D // 2
ROW_MASK, ROW_MAX = 96, 104
STACK = 120
GRID_W, GRID_H = 64, 32
SET_A, SET_B = (0, 1, 2), (3, 4)

FRONT, BACK = "front", "back"
STEPS = [
    (FRONT, "X"), (BACK, "AUX", 0), (FRONT, "Q", 0), (BACK, "S", 3, 0), (FRONT, "Q", 1), (BACK, "S", 3, 1),
    (FRONT, "Q", 2), (BACK, "S", 4, 0), (BACK, "ST", 0), (BACK, "S", 4, 1), (BACK, "ST", 1), (BACK, "AUX", 1),
    (BACK, "PV", 0), (BACK, "ST", 2), (BACK, "PV", 1), (FRONT, "Q", 3), (BACK, "PV", 2), (BACK, "ST", 3),
    (FRONT, "Q", 4), (BACK, "PV", 3), (BACK, "ST", 4), (BACK, "PV", 4), (FRONT, "S", 0, 0), (BACK, "AT", 0),
    (FRONT, "S", 0, 1), (BACK, "AT", 1), (FRONT, "S", 1, 0), (BACK, "O", 0, 0), (FRONT, "S", 1, 1),
    (BACK, "O", 0, 1), (FRONT, "S", 2, 0), (BACK, "O", 1, 0), (FRONT, "S", 2, 1), (BACK, "O", 1, 1),
]
X_CHUNKS = ((0, 2), (2, 4), (4, 5))
AT_CHUNKS = ((0, 4), (4, 5))
GENERAL = {"X": len(X_CHUNKS), "AUX": 1, "Q": 1, "AT": len(AT_CHUNKS), "O": 1}
SCORES = {"S": 2}


def uses(stage, table):
    return sum(table.get(s[1], 0) for s in STEPS if s[0] == stage)


GEN_F, GEN_B = uses(FRONT, GENERAL), uses(BACK, GENERAL)
SC_F, SC_B = uses(FRONT, SCORES), uses(BACK, SCORES)


class Iteration:

    def __init__(self, t, front, back, front_batch, back_batch):
        self.t, self.front, self.back = t, front, back
        self.batch = {FRONT: front_batch, BACK: back_batch}
        first = isinstance(t, int) and t == 0
        self.gen0 = 0 if first else t * (GEN_F + GEN_B) - GEN_B
        self.sc0 = 0 if first else t * (SC_F + SC_B) - SC_B

    def steps(self):
        gen = sc = 0
        for stage, kind, *args in STEPS:
            if (stage == FRONT and self.front) or (stage == BACK and self.back):
                yield stage, kind, args, gen, sc
                gen += GENERAL.get(kind, 0)
                sc += SCORES.get(kind, 0)

    def gen_after(self, kind, *args, use=0):
        for _, k, a, gen, _ in self.steps():
            if k == kind and tuple(a) == args:
                return self.gen0 + gen + use + 1


def iterations(engine, body):
    body(Iteration(0, True, False, 0, 0))
    with engine.Fori(1, PER_BATCH) as t:
        body(Iteration(t, True, True, 0, 0))
    body(Iteration(PER_BATCH, True, True, 1, 0))
    with engine.Fori(PER_BATCH + 1, BLOCKS - 1) as t:
        body(Iteration(t, True, True, 1, 1))
    body(Iteration(BLOCKS - 1, True, True, 1, 1))
    body(Iteration(BLOCKS, False, True, 1, 1))


def attention_kernel(nc, x, ctx, boxes, wq, wk, wv, wk_ip, wv_ip, wo, b_out,
                     c_ident, c_grid, c_rows, c_ones, c_pick, out):
    x_rows = x.rearrange("b s d -> (b s) d")
    out_rows = out.rearrange("b s d -> (b s) d")
    mask_dram = nc.dram_tensor("mask_scratch", (IP, BATCHES * SEQ), F32, kind="Internal").ap()

    with ExitStack() as stack:
        def sb(name, shape, dt=F32, where=stack):
            return where.enter_context(nc.sbuf_tensor(name, shape, dt))

        def sem(name):
            return stack.enter_context(nc.semaphore(name))

        ident = sb("ident", [P, P])
        wq_hi, wq_lo = sb("wq_hi", [P, KC, D], F32R), sb("wq_lo", [P, KC, D], F32R)
        wo_hi, wo_lo = sb("wo_hi", [P, KC, D], F32R), sb("wo_lo", [P, KC, D], F32R)
        k_stack = [sb(f"k_stack{b}", [P, HEADS, CTX], F32R) for b in range(BATCHES)]
        k_tail = [sb(f"k_tail{b}", [P, HEADS, P], F32R) for b in range(BATCHES)]
        v_main = [sb(f"v_main{b}", [P, HEADS, VW]) for b in range(BATCHES)]
        v_tail = [sb(f"v_tail{b}", [P, GROUPS, 8 * VW]) for b in range(BATCHES)]

        max_cols = [80, 16 * len(SET_B)]
        max_parts = [sb("max_parts_a", [P, QT, max_cols[0]], F32R), sb("max_parts_b", [P, QT, max_cols[1]], F32R)]

        with ExitStack() as setup:
            w_a, w_b = sb("w_a", [P, CC, D], where=setup), sb("w_b", [P, CC, D], where=setup)
            ctx_main = sb("ctx_main", [P, BATCHES, CTX_D], where=setup)
            ctx_rest = sb("ctx_rest", [P, CTX_D], where=setup)
            ctx_t = sb("ctx_t", [P, CC, BATCHES * CTX], where=setup)
            rest_t = sb("rest_t", [P, CC, BATCHES * TAIL], where=setup)
            w_raw = sb("w_raw", [P, KC, D], where=setup)
            k_hi = sb("k_hi", [P, GROUPS, BATCHES, CTX], F32R, setup)
            k_lo = sb("k_lo", [P, GROUPS, BATCHES, CTX], F32R, setup)
            row_consts = sb("row_consts", [P, 4 * CTX], where=setup)
            inside = sb("inside", [16, SEQ], BF16, setup)
            small = sb("small", [16, 256], where=setup)
            pick = sb("pick", [16, BATCHES * IP], BF16, setup)
        v_rest = ctx_main[0:BATCHES * REM, 0, 0:D]
        v_rest_ip = ctx_main[0:BATCHES * IP, 1, 0:D]
        mask = w_raw[0:IP, :, :].rearrange("p a b -> p (a b)")[:, 0:SEQ]

        x_in = sb("x_in", [P, QT, D])
        x_res = sb("x_res", [P, QT, D])
        bias = sb("bias", [P, D])
        xt_hi, xt_lo = sb("xt_hi", [P, KC, QB], F32R), sb("xt_lo", [P, KC, QB], F32R)
        q_hi, q_lo = sb("q_hi", [P, GROUPS, QB], F32R), sb("q_lo", [P, GROUPS, QB], F32R)
        q_stack = sb("q_stack", [P, HEADS, QB], F32R)
        neg_max = sb("neg_max", [P, QT, GROUPS, 8])
        aux_rows = [sb("aux_a", [16 * len(SET_A), QB], F32R), sb("aux_b", [16 * len(SET_B), QB], F32R)]
        p_main = sb("p_main", [P, 2, 4, QB])
        p_tail = sb("p_tail", [P, 2, QB])
        inv_den = sb("inv_den", [P, QT, 8])
        o_both = sb("o_both", [P, QT, 8, DH])
        attn = sb("attn", [P, QT, D])
        at_hi, at_lo = sb("at_hi", [P, QT, D], F32R), sb("at_lo", [P, QT, D], F32R)
        out_sb = sb("out_sb", [P, QT, D])

        bank = [stack.enter_context(nc.psum_tensor(f"bank{i}", [P, 512], F32)) for i in range(8)]
        general, scores, scores_t, product = bank[0:2], bank[2:4], bank[4:6], bank[6:8]

        s_ident, s_ctx, s_grid, s_rows = sem("ident_in"), sem("ctx_in"), sem("grid_in"), sem("rows_in")
        s_wk, s_wv, s_wq, s_wo, s_ones = sem("wk_in"), sem("wv_in"), sem("wq_in"), sem("wo_in"), sem("ones_in")
        s_bias = sem("bias_in")
        s_ctx_tr, s_ctx_t = sem("ctx_transposed"), sem("ctx_t_ready")
        s_kp, s_khi, s_klo, s_kst = sem("k_product"), sem("k_hi_ready"), sem("k_lo_ready"), sem("k_stack_in")
        s_vp, s_vc, s_vt = sem("v_product"), sem("v_copied"), sem("v_tail_in")
        s_fill, s_rowc, s_ktail = sem("filled"), sem("row_consts_copied"), sem("k_tail_ready")
        s_wsplit_hi, s_wsplit = sem("w_hi_ready"), sem("w_lo_ready")
        s_msk, s_cnt, s_mval, s_mout = sem("mask_chain"), sem("mask_counts"), sem("mask_values"), sem("mask_stored")
        x_loaded, xt_ready, xh_done = sem("x_loaded"), sem("x_transposed"), sem("xt_hi_ready")
        gen_freed = sem("general_bank_freed")
        q_ready, qh_done = sem("q_product"), sem("q_hi_ready")
        stack_in = [sem("stack_a_in"), sem("stack_b_in")]
        s_ready, s_freed = sem("scores_ready"), sem("maxima_taken")
        split_hi, split_done = sem("max_hi_ready"), [sem("max_a_split"), sem("max_b_split")]
        aux_ready, aux_in = sem("maxima_transposed"), [sem("aux_a_in"), sem("aux_b_in")]
        st_ready, exp_done = sem("scores_t_ready"), sem("exp_done")
        pv_ready, recip_done, norm_done, att_done = sem("pv_ready"), sem("recip_done"), sem("normalised"), sem("attn_ready")
        at_ready, ah_done = sem("attn_transposed"), sem("at_hi_ready")
        o_ready, stored = sem("out_product"), sem("out_stored")
        xr_loaded, xr_ready = sem("x_res_loaded"), sem("x_res_biased")

        STACK_PARTS = ((0, "hi"), (32, "lo"), (64, "hi"))
        K_PARTS = ((0, k_hi), (32, k_hi), (64, k_lo))
        N_STACK_DMAS = 4 * len(STACK_PARTS) + 1
        PRE_CTX = 5
        V_UNITS = [(b, c0, c1) for b in range(BATCHES) for c0, c1 in ((0, 512), (512, D))]
        VR_UNITS = [(ip, c0, c1) for ip in (0, 1) for c0, c1 in ((0, 512), (512, D))]

        block = stack.enter_context(nc.Block())

        @block.sync
        def _(sp):
            sp.dma_start(ctx_main[:], ctx[:, 0:P, :].rearrange("b p c -> p b c")).then_inc(s_ctx, 16)
            for b in range(BATCHES):
                sp.dma_start(ctx_rest[REM * b:REM * (b + 1), :], ctx[b, P:TEXT, :]).then_inc(s_ctx, 16)
                o = BATCHES * REM + IP * b
                sp.dma_start(ctx_rest[o:o + IP, :], ctx[b, TEXT:CTX, :]).then_inc(s_ctx, 16)
            sp.dma_start(ident[:], c_ident).then_inc(s_ident, 16)
            sp.dma_start(w_a[:], wk.rearrange("(c p) n -> p c n", p=P)).then_inc(s_wk, 16)
            sp.dma_start(w_b[:], wk_ip.rearrange("(c p) n -> p c n", p=P)).then_inc(s_wk, 16)
            sp.dma_start(row_consts[ROW_MASK:STACK, :], c_rows).then_inc(s_rows, 16)
            sp.dma_start(small[0:8, 0:4], boxes.rearrange("b m c -> (b m) c")).then_inc(s_grid, 16)
            sp.dma_start(small[0:8, 8:8 + GRID_W + GRID_H], c_grid).then_inc(s_grid, 16)
            sp.dma_start(small[0:9, 128:128 + BATCHES * IP], c_pick).then_inc(s_grid, 16)
            for b in range(BATCHES):
                for g in range(GROUPS):
                    sp.dma_start(v_tail[b][:, g, :], c_ones).then_inc(s_ones, 16)
            for b in range(BATCHES):
                sp.wait_ge(s_mval, 4 * (b + 1))
                sp.dma_start(mask_dram[:, b * SEQ:(b + 1) * SEQ], mask).then_inc(s_mout, 16)
            sp.wait_ge(s_mout, 16 * BATCHES)
            sp.dma_start(w_raw[:], wq.rearrange("(c p) n -> p c n", p=P)).then_inc(s_wq, 16)
            sp.wait_ge(s_kp, GROUPS)
            sp.dma_start(w_a[:], wv.rearrange("(c p) n -> p c n", p=P)).then_inc(s_wv, 16)
            sp.dma_start(w_b[:], wv_ip.rearrange("(c p) n -> p c n", p=P)).then_inc(s_wv, 16)
            sp.wait_ge(s_wsplit, 1)
            sp.dma_start(w_raw[:], wo.rearrange("(c p) n -> p c n", p=P)).then_inc(s_wo, 16)
            sp.wait_ge(s_klo, 2 * GROUPS)
            for b in range(BATCHES):
                for row, src in K_PARTS:
                    for j in range(4):
                        sp.dma_start(k_stack[b][row:row + DH, j:HEADS:4, :].bitcast(F32),
                                     src[DH * j:DH * (j + 1), :, b, :].bitcast(F32)).then_inc(s_kst, 16)
            sp.wait_ge(s_ones, 16 * BATCHES * GROUPS)
            sp.wait_ge(s_vc, len(V_UNITS) + len(VR_UNITS))
            for b in range(BATCHES):
                for j in range(4):
                    r = 32 * j
                    sp.dma_start(v_tail[b][r:r + REM, :, VW * j:VW * j + DH],
                                 v_rest[REM * b:REM * (b + 1), :].rearrange("p (g j d) -> p g j d", j=4, d=DH)[:, :, j, :]
                                 ).then_inc(s_vt, 16)
                    sp.dma_start(v_tail[b][r + REM:r + TAIL, :, VW * (4 + j):VW * (4 + j) + DH],
                                 v_rest_ip[IP * b:IP * (b + 1), :].rearrange("p (g j d) -> p g j d", j=4, d=DH)[:, :, j, :]
                                 ).then_inc(s_vt, 16)
            sp.wait_ge(s_vt, 16 * BATCHES * 8)
            sp.wait_ge(s_ktail, BATCHES * 4)
            sp.wait_ge(s_wsplit, 2)
            sp.dma_start(bias[:], b_out.rearrange("(a n) -> a n", a=1).to_broadcast([P, D])).then_inc(s_bias, 16)
            sp.dma_start(x_in[:], x_rows[0:QB, :].rearrange("(a p) d -> p a d", p=P)).then_inc(x_loaded, 16)

            def body(it):
                t = it.t
                if it.front and not (isinstance(t, int) and t == BLOCKS - 1):
                    sp.wait_ge(xt_ready, t * len(X_CHUNKS) + len(X_CHUNKS))
                    sp.dma_start(x_in[:], x_rows[bass.ds(t * QB + QB, QB), :].rearrange("(a p) d -> p a d", p=P)
                                 ).then_inc(x_loaded, 16)
                for n, groups in enumerate((SET_A, SET_B)):
                    if it.back:
                        sp.wait_ge(gen_freed, it.gen_after("AUX", n))
                        for i, g in enumerate(groups):
                            src = aux_rows[n][16 * i:16 * (i + 1), :].bitcast(F32).unsqueeze(1).to_broadcast([16, 4, QB])
                            sp.dma_start(q_stack[ROW_MAX:STACK, 4 * g:4 * g + 4, :].bitcast(F32), src
                                         ).then_inc(aux_in[n], 16)
                for n, groups in enumerate((SET_A, SET_B)):
                    g0, g1 = groups[0], groups[-1] + 1
                    if it.front:
                        sp.wait_ge(gen_freed, it.gen_after("Q", g1 - 1))
                        if it.back:
                            sp.wait_ge(st_ready, 15 * t - 15 + 3 * g1)
                        for row, part in STACK_PARTS:
                            src = q_hi if part == "hi" else q_lo
                            for j in range(4):
                                sp.dma_start(q_stack[row:row + DH, 4 * g0 + j:4 * g1:4, :].bitcast(F32),
                                             src[DH * j:DH * (j + 1), g0:g1, :].bitcast(F32)).then_inc(stack_in[n], 16)
                        src = mask_dram[:, bass.ds(t * QB, QB)].unsqueeze(1).to_broadcast([IP, 4 * len(groups), QB])
                        sp.dma_start(q_stack[ROW_MASK:ROW_MAX, 4 * g0:4 * g1, :].bitcast(F32), src
                                     ).then_inc(stack_in[n], 16)
                if it.back:
                    for qt in range(QT):
                        sp.wait_ge(gen_freed, it.gen_after("O", qt, 1))
                        sp.dma_start(out_rows[bass.ds(t * QB - QB + qt * P, P), :], out_sb[:, qt, :]).then_inc(stored, 16)
                    sp.wait_ge(stored, t * 16 * QT)
                if it.front:
                    sp.dma_start(x_res[:], x_rows[bass.ds(t * QB, QB), :].rearrange("(a p) d -> p a d", p=P)
                                 ).then_inc(xr_loaded, 16)

            iterations(sp, body)

        @block.gpsimd
        def _(pool):
            nc.gpsimd.memset(max_parts[0][:].bitcast(mybir.dt.uint32), 0).then_inc(s_fill, 1)
            for b in range(BATCHES):
                nc.gpsimd.memset(v_main[b][:], 1.0).then_inc(s_fill, 1)
            for b in range(BATCHES):
                nc.gpsimd.memset(k_tail[b][:].bitcast(mybir.dt.uint32), 0).then_inc(s_fill, 1)
            pool.wait_ge(s_bias, 16)

            def body(it):
                t = it.t
                if it.back:
                    pool.wait_ge(xr_loaded, t * 16)
                    nc.gpsimd.tensor_tensor(x_res[:], x_res[:], bias[:].unsqueeze(1).to_broadcast([P, QT, D]), ALU.add
                                            ).then_inc(xr_ready, 1)
                for stage, kind, args, gen, sc in it.steps():
                    if kind == "PV":
                        for qt in range(QT):
                            g = args[0]
                            pool.wait_ge(norm_done, t * 10 - 10 + 2 * g + qt + 1)
                            nc.gpsimd.tensor_tensor(attn[:, qt, P * g:P * (g + 1)].rearrange("p (h d) -> p h d", d=DH),
                                                    o_both[:, qt, 0:4, :], o_both[:, qt, 4:8, :], ALU.add
                                                    ).then_inc(att_done, 1)

            iterations(pool, body)

        @block.scalar
        def _(act):
            for g in range(GROUPS):
                act.wait_ge(s_kp, g + 1)
                ps = bank[(PRE_CTX + g) % 8]
                nc.scalar.activation(k_hi[:, g, :, 0:TEXT],
                                     ps[:, 0:BATCHES * TEXT].rearrange("p (b k) -> p b k", b=BATCHES),
                                     ACT.Copy, scale=SCALE).then_inc(s_khi, 1)
                nc.scalar.activation(k_hi[:, g, :, TEXT:CTX],
                                     ps[:, BATCHES * TEXT:BATCHES * CTX].rearrange("p (b k) -> p b k", b=BATCHES),
                                     ACT.Copy, scale=SCALE).then_inc(s_khi, 1)
                if g == 0:
                    act.wait_ge(s_wq, 16)
                    nc.scalar.activation(wq_hi[:], w_raw[:], ACT.Copy).then_inc(s_wsplit_hi, 1)
            act.wait_ge(s_fill, 1 + BATCHES)
            for n, (b, c0, c1) in enumerate(V_UNITS):
                act.wait_ge(s_vp, n + 1)
                h0, h1 = c0 // DH, c1 // DH
                nc.scalar.activation(v_main[b][:, h0:h1, 0:DH],
                                     bank[(PRE_CTX + GROUPS + n) % 8][:, 0:c1 - c0].rearrange("p (h d) -> p h d", d=DH),
                                     ACT.Copy).then_inc(s_vc, 1)
            for n, (ip, c0, c1) in enumerate(VR_UNITS):
                act.wait_ge(s_vp, len(V_UNITS) + n + 1)
                rows = BATCHES * (IP if ip else REM)
                nc.scalar.activation((v_rest_ip if ip else v_rest)[:, c0:c1],
                                     bank[(PRE_CTX + GROUPS + len(V_UNITS) + n) % 8][0:rows, 0:c1 - c0],
                                     ACT.Copy).then_inc(s_vc, 1)
            act.wait_ge(s_wo, 16)
            nc.scalar.activation(wo_hi[:], w_raw[:], ACT.Copy).then_inc(s_wsplit_hi, 1)

            def body(it):
                t = it.t
                for stage, kind, args, gen, sc in it.steps():
                    if kind == "X":
                        if it.back:
                            act.wait_ge(q_ready, t * GROUPS)
                        for u, (c0, c1) in enumerate(X_CHUNKS):
                            act.wait_ge(xt_ready, t * len(X_CHUNKS) + u + 1)
                            nc.scalar.activation(xt_hi[:, c0:c1, :].rearrange("p c q -> p (c q)"),
                                                 general[(gen + u) % 2][:, 0:(c1 - c0) * QB], ACT.Copy).then_inc(xh_done, 1)
                    if kind == "Q":
                        g = args[0]
                        n = 0 if g in SET_A else 1
                        act.wait_ge(q_ready, t * GROUPS + g + 1)
                        if it.back:
                            act.wait_ge(stack_in[n], t * (16 * N_STACK_DMAS))
                        nc.scalar.activation(q_hi[:, g, :], general[gen % 2][:, 0:QB], ACT.Copy).then_inc(qh_done, 1)
                    if kind == "ST":
                        g = args[0]
                        for u in range(3):
                            act.wait_ge(st_ready, t * 15 - 15 + 3 * g + u + 1)
                            src = scores_t[(3 * g + u) % 2]
                            if u < 2:
                                dst = p_main[:, g % 2, 2 * u:2 * u + 2, :].rearrange("p h q -> p (h q)")
                                nc.scalar.activation(dst, src[:], ACT.Exp).then_inc(exp_done, 1)
                            else:
                                nc.scalar.activation(p_tail[:, g % 2, :], src[:, 0:QB], ACT.Exp).then_inc(exp_done, 1)
                    if kind == "AT":
                        qt = args[0]
                        for u, (c0, c1) in enumerate(AT_CHUNKS):
                            act.wait_ge(at_ready, t * 4 - 4 + 2 * qt + u + 1)
                            nc.scalar.activation(at_hi[:, qt, P * c0:P * c1], general[(gen + u) % 2][:, 0:P * (c1 - c0)],
                                                 ACT.Copy).then_inc(ah_done, 1)

            iterations(act, body)

        @block.vector
        def _(dve):
            box, xs, ys = small[0:8, 0:4], small[0:8, 8:8 + GRID_W], small[0:8, 8 + GRID_W:8 + GRID_W + GRID_H]
            gx, gy = small[0:8, 144:144 + GRID_W], small[0:8, 208:208 + GRID_H]
            dve.wait_ge(s_grid, 48)
            nc.vector.tensor_copy(pick[0:9, :], small[0:9, 128:128 + BATCHES * IP])
            nc.vector.memset(inside[0:9, :], 1.0)
            nc.vector.tensor_scalar(gx, xs, box[:, 0:1], None, ALU.is_ge)
            nc.vector.tensor_scalar(gy, ys, box[:, 1:2], None, ALU.is_ge).then_inc(s_msk, 1)
            dve.wait_ge(s_msk, 1)
            nc.vector.scalar_tensor_tensor(out=gx, in0=xs, scalar=box[:, 2:3], in1=gx, op0=ALU.is_le, op1=ALU.mult)
            nc.vector.scalar_tensor_tensor(out=gy, in0=ys, scalar=box[:, 3:4], in1=gy, op0=ALU.is_le, op1=ALU.mult
                                           ).then_inc(s_msk, 1)
            dve.wait_ge(s_msk, 2)
            nc.vector.tensor_tensor(inside[0:8, :].rearrange("p (y x) -> p y x", x=GRID_W),
                                    gy.unsqueeze(2).to_broadcast([8, GRID_H, GRID_W]),
                                    gx.unsqueeze(1).to_broadcast([8, GRID_H, GRID_W]), ALU.mult).then_inc(s_msk, 1)
            for b in range(BATCHES):
                for half in range(2):
                    u = 2 * b + half
                    dve.wait_ge(s_ctx_tr, u + 1)
                    nc.vector.tensor_copy(ctx_t[:, 4 * half:4 * half + 4, b * TEXT:b * TEXT + P],
                                          bank[u][:].rearrange("p (c k) -> p c k", c=4)).then_inc(s_ctx_t, 1)
            dve.wait_ge(s_ctx_tr, 5)
            rest = bank[4][:, 0:CC * BATCHES * TAIL].rearrange("p (c k) -> p c k", c=CC)
            nc.vector.tensor_copy(rest_t[:], rest)
            for b in range(BATCHES):
                nc.vector.tensor_copy(ctx_t[:, :, b * TEXT + P:(b + 1) * TEXT], rest[:, :, b * REM:(b + 1) * REM])
            nc.vector.tensor_copy(ctx_t[:, :, BATCHES * TEXT:], rest[:, :, BATCHES * REM:]).then_inc(s_ctx_t, 1)
            for n in range(2 * 4):
                b, c = n // 4, n % 4
                dve.wait_ge(s_cnt, n + 1)
                if n == 4:
                    dve.wait_ge(s_mout, 16)
                nc.vector.tensor_scalar(mask[:, 512 * c:512 * (c + 1)], bank[n % 2][0:IP, :], -1.0, -NEG,
                                        ALU.max, ALU.mult).then_inc(s_mval, 1)
            dve.wait_ge(s_rows, 16)
            for b in range(BATCHES):
                nc.vector.tensor_copy(k_stack[b][ROW_MASK:STACK, :, :].rearrange("p (g j) k -> p g (j k)", j=4),
                                      row_consts[ROW_MASK:STACK, :].unsqueeze(1).to_broadcast([STACK - ROW_MASK, GROUPS, 4 * CTX])
                                      ).then_inc(s_rowc, 1)
            for g in range(GROUPS):
                ps = bank[(PRE_CTX + g) % 8]
                dve.wait_ge(s_khi, 2 * g + 2)
                for u, (c0, c1, k0, k1) in enumerate(((0, BATCHES * TEXT, 0, TEXT),
                                                      (BATCHES * TEXT, BATCHES * CTX, TEXT, CTX))):
                    for b in range(BATCHES):
                        w = (c1 - c0) // BATCHES
                        last = nc.vector.scalar_tensor_tensor(
                            out=k_lo[:, g, b, k0:k1], in0=ps[:, c0 + b * w:c0 + (b + 1) * w], scalar=SCALE,
                            in1=k_hi[:, g, b, k0:k1].bitcast(F32), op0=ALU.mult, op1=ALU.subtract)
                    last.then_inc(s_klo, 1)
            dve.wait_ge(s_wsplit_hi, 1)
            nc.vector.tensor_tensor(wq_lo[:], w_raw[:], wq_hi[:].bitcast(F32), ALU.subtract).then_inc(s_wsplit, 1)
            dve.wait_ge(s_fill, 1 + 2 * BATCHES)
            dve.wait_ge(s_kst, 16 * 24)
            dve.wait_ge(s_rowc, BATCHES)
            for b in range(BATCHES):
                for j in range(4):
                    nc.vector.tensor_copy(k_tail[b][0:STACK, j:HEADS:4, 32 * j:32 * j + TAIL],
                                          k_stack[b][0:STACK, j:HEADS:4, P:CTX].bitcast(F32)).then_inc(s_ktail, 1)
            dve.wait_ge(s_wsplit_hi, 2)
            nc.vector.tensor_tensor(wo_lo[:], w_raw[:], wo_hi[:].bitcast(F32), ALU.subtract).then_inc(s_wsplit, 1)

            def body(it):
                t = it.t
                for stage, kind, args, gen, sc in it.steps():
                    if kind == "X":
                        for u, (c0, c1) in enumerate(X_CHUNKS):
                            dve.wait_ge(xh_done, t * len(X_CHUNKS) + u + 1)
                            nc.vector.tensor_tensor(xt_lo[:, c0:c1, :].rearrange("p c q -> p (c q)"),
                                                    general[(gen + u) % 2][:, 0:(c1 - c0) * QB],
                                                    xt_hi[:, c0:c1, :].bitcast(F32).rearrange("p c q -> p (c q)"),
                                                    ALU.subtract).then_inc(gen_freed, 1)
                    if kind == "Q":
                        g = args[0]
                        dve.wait_ge(qh_done, t * GROUPS + g + 1)
                        nc.vector.tensor_tensor(q_lo[:, g, :], general[gen % 2][:, 0:QB], q_hi[:, g, :].bitcast(F32),
                                                ALU.subtract).then_inc(gen_freed, 1)
                    if kind == "S":
                        g, qt = args
                        for pair in range(2):
                            dve.wait_ge(s_ready, it.sc0 + sc + pair + 1)
                            src = scores[(sc + pair) % 2][:, 0:2 * CTX].rearrange("p (h k) -> p h k", h=2)
                            dst = neg_max[:, qt, g, 4 * pair:4 * pair + 4].rearrange("p (h s) -> p h s", s=2)
                            nc.vector.tensor_reduce(dst[:, :, 0], src[:, :, 0:TEXT], AX_X, ALU.max, negate=True)
                            nc.vector.tensor_reduce(dst[:, :, 1], src[:, :, TEXT:CTX], AX_X, ALU.max, negate=True
                                                    ).then_inc(s_freed, 1)
                        for n, groups in enumerate((SET_A, SET_B)):
                            if (g, qt) == (groups[-1], QT - 1):
                                c0, c1 = 8 * groups[0], 8 * (groups[-1] + 1)
                                parts = max_parts[n][:, :, 0:2 * (c1 - c0)].rearrange("p a (m e) -> p a m e", e=2)
                                whole = neg_max[:].rearrange("p a g e -> p a (g e)")[:, :, c0:c1]
                                dve.wait_ge(s_freed, it.sc0 + sc + 2)
                                nc.vector.tensor_copy(parts[:, :, :, 0], whole).then_inc(split_hi, 1)
                                dve.wait_ge(split_hi, t * 2 + (1 if n == 0 else 0))
                                nc.vector.tensor_tensor(parts[:, :, :, 1], whole, parts[:, :, :, 0].bitcast(F32),
                                                        ALU.subtract).then_inc(split_done[n], 1)
                    if kind == "AUX":
                        n = args[0]
                        dve.wait_ge(aux_ready, t * 2 - 2 + n + 1)
                        nc.vector.tensor_copy(aux_rows[n][:], general[gen % 2][0:aux_rows[n].shape[0], 0:QB]
                                              ).then_inc(gen_freed, 1)
                    if kind == "PV":
                        g = args[0]
                        for qt in range(QT):
                            n = t * 10 - 10 + 2 * g + qt
                            dve.wait_ge(pv_ready, n + 1)
                            both = product[qt][:, 0:8 * VW].rearrange("p (e d) -> p e d", d=VW)
                            nc.vector.reciprocal(inv_den[:, qt, :], both[:, :, DH]).then_inc(recip_done, 1)
                            dve.wait_ge(recip_done, n + 1)
                            if g > 0:
                                dve.wait_ge(att_done, n - 1)
                            nc.vector.tensor_tensor(o_both[:, qt, :, :], both[:, :, 0:DH],
                                                    inv_den[:, qt, :].unsqueeze(2).to_broadcast([P, 8, DH]), ALU.mult
                                                    ).then_inc(norm_done, 1)
                    if kind == "AT":
                        qt = args[0]
                        for u, (c0, c1) in enumerate(AT_CHUNKS):
                            dve.wait_ge(ah_done, t * 4 - 4 + 2 * qt + u + 1)
                            nc.vector.tensor_tensor(at_lo[:, qt, P * c0:P * c1], general[(gen + u) % 2][:, 0:P * (c1 - c0)],
                                                    at_hi[:, qt, P * c0:P * c1].bitcast(F32), ALU.subtract
                                                    ).then_inc(gen_freed, 1)
                    if kind == "O":
                        qt, half = args
                        if (qt, half) == (0, 0):
                            dve.wait_ge(xr_ready, t + 0)
                        dve.wait_ge(o_ready, t * 4 - 4 + 2 * qt + half + 1)
                        cols = slice(HALF * half, HALF * (half + 1))
                        last = nc.vector.tensor_tensor(out_sb[:, qt, cols], general[gen % 2][:, 0:HALF], x_res[:, qt, cols],
                                                       ALU.add)
                        last.then_inc(gen_freed, 1)

            iterations(dve, body)

        @block.tensor
        def _(pe):
            pe.wait_ge(s_ident, 16)
            pe.wait_ge(s_ctx, 16 * 5)
            for b in range(BATCHES):
                for half in range(2):
                    for c in range(4):
                        last = nc.tensor.transpose(bank[2 * b + half][:, P * c:P * (c + 1)],
                                                   ctx_main[:, b, P * (4 * half + c):P * (4 * half + c + 1)], ident[:])
                    last.then_inc(s_ctx_tr, 1)
            n = BATCHES * TAIL
            for c in range(CC):
                last = nc.tensor.transpose(bank[4][:, n * c:n * (c + 1)], ctx_rest[0:n, P * c:P * (c + 1)], ident[0:n, 0:n])
            last.then_inc(s_ctx_tr, 1)
            pe.wait_ge(s_msk, 3)
            pe.wait_ge(s_ctx_t, 5)
            for n in range(2 * 4):
                b, c = n // 4, n % 4
                if n >= 2:
                    pe.wait_ge(s_mval, n - 1)
                nc.tensor.matmul(bank[n % 2][0:IP, :], pick[0:9, IP * b:IP * (b + 1)], inside[0:9, 512 * c:512 * (c + 1)],
                                 start=True, stop=True).then_inc(s_cnt, 1)
            pe.wait_ge(s_wk, 32)
            pe.wait_ge(s_mval, 8)
            text, both = BATCHES * TEXT, BATCHES * CTX
            for g in range(GROUPS):
                ps = bank[(PRE_CTX + g) % 8]
                for c in range(CC):
                    nc.tensor.matmul(ps[:, 0:text], w_a[:, c, P * g:P * (g + 1)], ctx_t[:, c, 0:text],
                                     start=(c == 0), stop=(c == CC - 1))
                for c in range(CC):
                    last = nc.tensor.matmul(ps[:, text:both], w_b[:, c, P * g:P * (g + 1)], ctx_t[:, c, text:both],
                                            start=(c == 0), stop=(c == CC - 1))
                last.then_inc(s_kp, 1)
            pe.wait_ge(s_wv, 32)
            for n, (b, c0, c1) in enumerate(V_UNITS):
                if n + GROUPS >= 8:
                    pe.wait_ge(s_klo, 2 * (n + GROUPS - 7))
                for c in range(CC):
                    last = nc.tensor.matmul(bank[(PRE_CTX + GROUPS + n) % 8][:, 0:c1 - c0],
                                            ctx_t[:, c, b * TEXT:b * TEXT + P], w_a[:, c, c0:c1],
                                            start=(c == 0), stop=(c == CC - 1))
                last.then_inc(s_vp, 1)
            for n, (ip, c0, c1) in enumerate(VR_UNITS):
                pe.wait_ge(s_klo, 2 * min(GROUPS, n + len(V_UNITS) + GROUPS - 7))
                r0, r1 = (BATCHES * REM, BATCHES * TAIL) if ip else (0, BATCHES * REM)
                for c in range(CC):
                    last = nc.tensor.matmul(bank[(PRE_CTX + GROUPS + len(V_UNITS) + n) % 8][0:r1 - r0, 0:c1 - c0],
                                            rest_t[:, c, r0:r1], (w_b if ip else w_a)[:, c, c0:c1],
                                            start=(c == 0), stop=(c == CC - 1))
                last.then_inc(s_vp, 1)

            def free_general(it, gen, u=0):
                if it.back or gen + u >= 2:
                    pe.wait_ge(gen_freed, it.gen0 + gen + u - 1)

            def split_product(ps, lhs_hi, lhs_lo, rhs_hi, rhs_lo):
                terms = [(l, r, c) for c in range(KC) for l, r in ((lhs_hi, rhs_hi), (lhs_lo, rhs_hi), (lhs_hi, rhs_lo))]
                for i, (l, r, c) in enumerate(terms):
                    last = nc.tensor.matmul(ps, l(c), r(c), start=(i == 0), stop=(i == len(terms) - 1))
                return last

            def body(it):
                t = it.t
                for stage, kind, args, gen, sc in it.steps():
                    batch = it.batch[stage]
                    if kind == "X":
                        pe.wait_ge(x_loaded, t * 16 + 16)
                        for u, (c0, c1) in enumerate(X_CHUNKS):
                            free_general(it, gen, u)
                            for c in range(c0, c1):
                                for qt in range(QT):
                                    at = (c - c0) * QB + qt * P
                                    last = nc.tensor.transpose(general[(gen + u) % 2][:, at:at + P],
                                                               x_in[:, qt, P * c:P * (c + 1)], ident[:])
                            last.then_inc(xt_ready, 1)
                    if kind == "Q":
                        g = args[0]
                        if g == 0:
                            pe.wait_ge(gen_freed, it.gen_after("X", use=len(X_CHUNKS) - 1))
                        free_general(it, gen)
                        cols = slice(P * g, P * (g + 1))
                        split_product(general[gen % 2][:, 0:QB],
                                      lambda c: wq_hi[:, c, cols], lambda c: wq_lo[:, c, cols],
                                      lambda c: xt_hi[:, c, :], lambda c: xt_lo[:, c, :]).then_inc(q_ready, 1)
                    if kind == "S":
                        g, qt = args
                        if qt == 0 and g in (SET_A[0], SET_B[0]):
                            n = 0 if g in SET_A else 1
                            blocks = t + 1 if stage == FRONT else t + 0
                            pe.wait_ge(stack_in[n], blocks * (16 * N_STACK_DMAS))
                        for pair in range(2):
                            if it.back or sc + pair >= 2:
                                pe.wait_ge(s_freed, it.sc0 + sc + pair - 1)
                            for i in range(2):
                                h = 4 * g + 2 * pair + i
                                last = nc.tensor.matmul(scores[(sc + pair) % 2][:, i * CTX:(i + 1) * CTX],
                                                        q_stack[0:ROW_MAX, h, P * qt:P * (qt + 1)],
                                                        k_stack[batch][0:ROW_MAX, h, :], start=True, stop=True)
                            last.then_inc(s_ready, 1)
                    if kind == "AUX":
                        n = args[0]
                        pe.wait_ge(split_done[n], t + 0)
                        free_general(it, gen)
                        for qt in range(QT):
                            last = nc.tensor.transpose(general[gen % 2][0:max_cols[n], P * qt:P * (qt + 1)],
                                                       max_parts[n][:, qt, :].bitcast(F32), ident[:])
                        last.then_inc(aux_ready, 1)
                    if kind == "ST":
                        g = args[0]
                        if g in (SET_A[0], SET_B[0]):
                            n = 0 if g in SET_A else 1
                            pe.wait_ge(aux_in[n], t * (16 * len((SET_A, SET_B)[n])))
                        for u in range(3):
                            if g or u > 1:
                                pe.wait_ge(exp_done, t * 15 - 15 + 3 * g + u - 1)
                            ps = scores_t[(3 * g + u) % 2]
                            if u < 2:
                                for i in range(2):
                                    h = 4 * g + 2 * u + i
                                    last = nc.tensor.matmul(ps[:, QB * i:QB * (i + 1)], k_stack[batch][0:STACK, h, 0:P],
                                                            q_stack[0:STACK, h, :], start=True, stop=True)
                            else:
                                for i in range(4):
                                    h = 4 * g + i
                                    last = nc.tensor.matmul(ps[:, 0:QB], k_tail[batch][0:STACK, h, :],
                                                            q_stack[0:STACK, h, :], start=(i == 0), stop=(i == 3))
                            last.then_inc(st_ready, 1)
                    if kind == "PV":
                        g = args[0]
                        pe.wait_ge(exp_done, t * 15 - 15 + 3 * g + 3)
                        for qt in range(QT):
                            if g > 0:
                                pe.wait_ge(norm_done, t * 10 - 10 + 2 * g + qt - 1)
                            queries = slice(P * qt, P * (qt + 1))
                            nc.tensor.matmul(product[qt][:, 0:8 * VW], p_tail[:, g % 2, queries], v_tail[batch][:, g, :],
                                             start=True, stop=False)
                            for j in range(4):
                                last = nc.tensor.matmul(product[qt][:, VW * j:VW * (j + 1)], p_main[:, g % 2, j, queries],
                                                        v_main[batch][:, 4 * g + j, :], start=False, stop=(j == 3))
                            last.then_inc(pv_ready, 1)
                    if kind == "AT":
                        qt = args[0]
                        pe.wait_ge(att_done, t * 10 - 1 + qt)
                        for u, (c0, c1) in enumerate(AT_CHUNKS):
                            free_general(it, gen, u)
                            for c in range(c0, c1):
                                last = nc.tensor.transpose(general[(gen + u) % 2][:, P * (c - c0):P * (c - c0 + 1)],
                                                           attn[:, qt, P * c:P * (c + 1)], ident[:])
                            last.then_inc(at_ready, 1)
                    if kind == "O":
                        qt, half = args
                        if half == 0:
                            pe.wait_ge(gen_freed, it.gen_after("AT", qt, use=len(AT_CHUNKS) - 1))
                        free_general(it, gen)
                        cols = slice(HALF * half, HALF * (half + 1))
                        split_product(general[gen % 2][:, 0:HALF],
                                      lambda c: at_hi[:, qt, P * c:P * (c + 1)], lambda c: at_lo[:, qt, P * c:P * (c + 1)],
                                      lambda c: wo_hi[:, c, cols], lambda c: wo_lo[:, c, cols]).then_inc(o_ready, 1)

            iterations(pe, body)


_INS = ["x", "ctx_2048", "fside_Bx4x4_0", "L0_xattn_w_q", "L0_xattn_w_k", "L0_xattn_w_v",
        "L0_xattn_w_k_ip", "L0_xattn_w_v_ip", "L0_xattn_w_out", "L0_xattn_b_out"]


def shape_constants():
    grid = np.zeros((8, GRID_W + GRID_H), np.float32)
    grid[:, :GRID_W] = np.linspace(0.0, 1.0, GRID_W, dtype=np.float32)
    grid[:, GRID_W:] = np.linspace(0.0, 1.0, GRID_H, dtype=np.float32)
    rows = np.zeros((STACK - ROW_MASK, 4, CTX), np.float32)
    for r in range(IP):
        rows[r, :, TEXT + r] = 1.0
    for j in range(4):
        rows[IP + 4 * j:IP + 4 * j + 2, j, :TEXT] = 1.0
        rows[IP + 4 * j + 2:IP + 4 * j + 4, j, TEXT:] = 1.0
    ones = np.zeros((P, 8, VW), np.float32)
    for j in range(4):
        ones[32 * j:32 * j + REM, j, DH] = 1.0
        ones[32 * j + REM:32 * j + TAIL, 4 + j, DH] = 1.0
    pick = np.zeros((9, BATCHES, IP), np.float32)
    for b in range(BATCHES):
        for m in range(4):
            pick[4 * b + m, b, :DUMMIES] = -1.0
            pick[4 * b + m, b, DUMMIES + m] = 1.0
        pick[8, b, DUMMIES:] = -1.0
    return {"identity": np.eye(P, dtype=np.float32), "grid": grid, "stack_rows": rows.reshape(STACK - ROW_MASK, -1),
            "tail_ones": ones.reshape(P, -1), "mask_pick": pick.reshape(9, -1)}


def kernel(**inputs):
    import concourse.bacc as bacc
    from concourse.bass_utils import run_bass_kernel_spmd

    nc = bacc.Bacc("TRN2", target_bir_lowering=False, num_devices=1)
    arrays = {f"in_{name}": np.ascontiguousarray(inputs[name]) for name in _INS}
    arrays |= {f"const_{name}": a for name, a in shape_constants().items()}
    args = [nc.dram_tensor(name, a.shape, mybir.dt.from_np(a.dtype), kind="ExternalInput").ap()
            for name, a in arrays.items()]
    out = nc.dram_tensor("out_0", (BATCHES, SEQ, D), F32, kind="ExternalOutput").ap()
    attention_kernel(nc, *args, out)
    r = run_bass_kernel_spmd(nc, [arrays], core_ids=[0])
    return r.results[0]["out_0"]
```

```python
from contextlib import ExitStack

import numpy as np

import concourse.bass as bass
from concourse import mybir

F32 = mybir.dt.float32
F32R = mybir.dt.float32r
BF16 = mybir.dt.bfloat16
ALU = mybir.AluOpType
ACT = mybir.ActivationFunctionType
AX_X = mybir.AxisListType.X

P = 128
BATCHES, SEQ, D = 2, 2048, 640
CTX, CTX_D = 154, 1024
HEADS, DH = 20, 32
IP = 8
DUMMIES = 4
TEXT = CTX - IP
REM = TEXT - P
TAIL = REM + IP
NEG = -10000.0
SCALE = float(np.float32(1.0) / np.sqrt(np.float32(DH)))

KC = D // P
CC = CTX_D // P
GROUPS = HEADS // 4
QB = 256
QT = QB // P
BLOCKS = BATCHES * SEQ // QB
PER_BATCH = BLOCKS // BATCHES
VW = DH + 1
HALF = D // 2
ROW_MASK, ROW_MAX = 96, 104
STACK = 120
GRID_W, GRID_H = 64, 32
SET_A, SET_B = (0, 1, 2), (3, 4)

FRONT, BACK, NEXT = "front", "back", "next"
STEPS = [
    (BACK, "AUX", 0), (BACK, "S", 3, 0), (FRONT, "Q", 0), (BACK, "S", 3, 1), (FRONT, "Q", 1), (BACK, "S", 4, 0),
    (FRONT, "Q", 2), (BACK, "S", 4, 1), (FRONT, "Q", 3), (BACK, "ST", 0, 0), (BACK, "ST", 0, 1), (BACK, "AUX", 1),
    (FRONT, "Q", 4), (BACK, "ST", 0, 2),
    (BACK, "ST", 1, 0), (BACK, "ST", 1, 1), (BACK, "PV", 0, 0), (BACK, "ST", 1, 2), (BACK, "PV", 0, 1),
    (BACK, "ST", 2, 0), (BACK, "ST", 2, 1), (BACK, "PV", 1, 0), (BACK, "ST", 2, 2), (BACK, "PV", 1, 1),
    (BACK, "ST", 3, 0), (BACK, "ST", 3, 1), (BACK, "PV", 2, 0), (BACK, "ST", 3, 2), (BACK, "PV", 2, 1),
    (BACK, "ST", 4, 0), (BACK, "ST", 4, 1), (BACK, "PV", 3, 0), (BACK, "ST", 4, 2), (BACK, "PV", 3, 1),
    (NEXT, "X", 0), (BACK, "PV", 4, 0), (BACK, "PV", 4, 1), (FRONT, "S", 0, 0), (NEXT, "X", 1), (FRONT, "S", 0, 1),
    (BACK, "AT", 0), (FRONT, "S", 1, 0), (BACK, "AT", 1), (BACK, "O", 0, 0), (FRONT, "S", 1, 1), (NEXT, "X", 2),
    (BACK, "O", 0, 1), (FRONT, "S", 2, 0), (BACK, "O", 1, 0), (FRONT, "S", 2, 1), (BACK, "O", 1, 1),
]
X_CHUNKS = ((0, 2), (2, 4), (4, 5))
NX = len(X_CHUNKS)
AT_CHUNKS = ((0, 4), (4, 5))

V_UNITS = [(keys, c0, c1) for keys in ("ip", "rest", "batch 0", "batch 1") for c0, c1 in ((0, 512), (512, D))]
V_PLACES = {("X", 0): (0, 1), ("S", 1, 0): (2, 3), ("S", 2, 0): (4, 5), None: (6, 7)}
W_O_PLACE = ("S", 2, 0)
COUNTS = {0: (0, 3), 1: (3, 4), 3: (4, 7), 4: (7, 8)}
GENERAL = {"X": 1, "AUX": 1, "Q": 1}
SCORES = {"S": 2}


def uses(stage, table):
    return sum(table.get(s[1], 0) for s in STEPS if s[0] == stage)


GEN_F, GEN_B, GEN_N = (uses(stage, GENERAL) for stage in (FRONT, BACK, NEXT))
SC_F, SC_B = uses(FRONT, SCORES), uses(BACK, SCORES)
GEN_ALL = GEN_F + GEN_B + GEN_N


class Iteration:

    def __init__(self, t, stages, front_batch, back_batch):
        self.t, self.stages = t, stages
        self.front, self.back, self.next = (stage in stages for stage in (FRONT, BACK, NEXT))
        self.batch = {FRONT: front_batch, BACK: back_batch, NEXT: None}
        if isinstance(t, int) and t == 0:
            self.gen0, self.sc0 = GEN_N, 0
        else:
            self.gen0, self.sc0 = t * GEN_ALL + (GEN_N - GEN_B), t * (SC_F + SC_B) - SC_B
            if isinstance(t, int) and t == BLOCKS:
                self.gen0 -= GEN_N
        self.parity = (self.gen0 if isinstance(t, int) else GEN_N - GEN_B) % 2

    def steps(self):
        gen = sc = 0
        for stage, kind, *args in STEPS:
            if stage in self.stages:
                yield stage, kind, args, gen, sc
                gen += GENERAL.get(kind, 0)
                sc += SCORES.get(kind, 0)

    def gen_after(self, kind, *args, use=0):
        for _, k, a, gen, _ in self.steps():
            if k == kind and tuple(a) == args:
                return self.gen0 + gen + use + 1


def iterations(engine, body):
    body(Iteration(0, (FRONT, NEXT), 0, 0))
    with engine.Fori(1, PER_BATCH) as t:
        body(Iteration(t, (FRONT, BACK, NEXT), 0, 0))
    body(Iteration(PER_BATCH, (FRONT, BACK, NEXT), 1, 0))
    with engine.Fori(PER_BATCH + 1, BLOCKS - 1) as t:
        body(Iteration(t, (FRONT, BACK, NEXT), 1, 1))
    body(Iteration(BLOCKS - 1, (FRONT, BACK), 1, 1))
    body(Iteration(BLOCKS, (BACK,), 1, 1))


def attention_kernel(nc, x, ctx, boxes, wq, wk, wv, wk_ip, wv_ip, wo, b_out,
                     c_ident, c_grid, c_rows, c_ones, c_pick, out):
    x_rows = x.rearrange("b s d -> (b s) d")
    out_rows = out.rearrange("b s d -> (b s) d")
    mask_dram = nc.dram_tensor("mask_scratch", (IP, BATCHES * SEQ), F32, kind="Internal").ap()

    with ExitStack() as stack:
        def sb(name, shape, dt=F32, where=stack):
            return where.enter_context(nc.sbuf_tensor(name, shape, dt))

        def sem(name):
            return stack.enter_context(nc.semaphore(name))

        ident = sb("ident", [P, P])
        with ExitStack() as setup:
            wq_raw, wo_raw = sb("wq_raw", [P, KC, D], where=setup), sb("wo_raw", [P, 2 * KC, D], where=setup)
        wq_lo = sb("wq_lo", [P, KC, D], F32R)
        wo_both = sb("wo_both", [P, 2 * KC, D], F32R)
        wo_hi, wo_lo = wo_both[:, 0:KC, :], wo_both[:, KC:2 * KC, :]
        wq_hi = sb("wq_hi", [P, KC, D], F32R)
        k_stack = [sb(f"k_stack{b}", [P, HEADS, CTX], F32R) for b in range(BATCHES)]
        k_tail = [sb(f"k_tail{b}", [P, HEADS, P], F32R) for b in range(BATCHES)]
        v_main = [sb(f"v_main{b}", [P, HEADS, VW]) for b in range(BATCHES)]
        v_tail = [sb(f"v_tail{b}", [P, GROUPS, 8 * VW]) for b in range(BATCHES)]
        max_cols = [80, 16 * len(SET_B)]
        max_parts = [sb("max_parts_a", [P, QT, max_cols[0]], F32R), sb("max_parts_b", [P, QT, max_cols[1]], F32R)]
        neg_max = sb("neg_max", [P, QT, GROUPS, 8])
        x_in = sb("x_in", [P, QT, D])

        with ExitStack() as setup:
            ctx_main = sb("ctx_main", [P, BATCHES, CTX_D], where=setup)
            ctx_rest = sb("ctx_rest", [P, CTX_D], where=setup)
            mask = sb("mask", [IP, SEQ], where=setup)
            w_k_ip = sb("w_k_ip", [P, CC, D], where=setup)
            w_kv = sb("w_kv", [P, CC, D], where=setup)
            ctx_t = sb("ctx_t", [P, CC, BATCHES * CTX], where=setup)
            rest_t = sb("rest_t", [P, CC, BATCHES * TAIL], where=setup)
            small = sb("small", [16, 256], where=setup)
            pick = sb("pick", [16, BATCHES * IP], BF16, setup)
            with ExitStack() as first:
                row_raw = sb("row_raw", [STACK - ROW_MASK, 4 * CTX], where=first)
                row_consts = sb("row_consts", [STACK - ROW_MASK, 4 * CTX], F32R, first)
            v_rest = sb("v_rest", [BATCHES * REM, D], where=setup)
            v_rest_ip = sb("v_rest_ip", [BATCHES * IP, D], where=setup)
        w_v_ip = wo_raw[:, 0:CC, :]
        inside = wo_raw[0:9, CC:2 * KC, :].bitcast(BF16).rearrange("p a b -> p (a b)")[:, 0:SEQ]
        k_hi, k_lo = (k_tail[i][:].rearrange("p h k -> p (h k)")[:, 0:GROUPS * BATCHES * CTX]
                      .rearrange("p (g b k) -> p g b k", g=GROUPS, b=BATCHES) for i in range(2))

        xt_hi, xt_lo = sb("xt_hi", [P, KC, QB], F32R), sb("xt_lo", [P, KC, QB], F32R)
        q_hi, q_lo = sb("q_hi", [P, GROUPS, QB], F32R), sb("q_lo", [P, GROUPS, QB], F32R)
        q_stack = sb("q_stack", [P, HEADS, QB], F32R)
        aux_rows = [sb("aux_a", [16 * len(SET_A), QB], F32R), sb("aux_b", [16 * len(SET_B), QB], F32R)]
        p_main = sb("p_main", [P, 2, 4, QB])
        p_tail = sb("p_tail", [P, 2, QB])
        inv_den = sb("inv_den", [P, QT, 8])
        o_both = sb("o_both", [P, QT, 8, DH])
        attn = sb("attn", [P, QT, D])
        bias = sb("bias", [P, D])
        x_res = sb("x_res", [P, QT, D])
        at_hi, at_lo = sb("at_hi", [P, QT, D], F32R), sb("at_lo", [P, QT, D], F32R)
        out_sb = sb("out_sb", [P, QT, D])

        bank = [stack.enter_context(nc.psum_tensor(f"bank{i}", [P, 512], F32)) for i in range(8)]
        general, scores, scores_t, product = bank[0:2], bank[2:4], bank[4:6], bank[6:8]

        s_ident, s_ctx, s_grid, s_rows = sem("ident_in"), sem("ctx_in"), sem("grid_in"), sem("stack_rows_in")
        s_ones_row = sem("ones_row_filled")
        s_row_raw, s_row_consts = sem("row_consts_in"), sem("row_consts_ready")
        s_wk = [sem(f"wk_in{g}") for g in range(GROUPS)]
        s_wv, s_wv_ip, s_wq, s_wo = sem("wv_in"), sem("wv_ip_in"), sem("wq_in"), sem("wo_in")
        s_ones, s_bias, s_fill, s_ktail_zero = sem("ones_in"), sem("bias_in"), sem("filled"), sem("k_tail_zero")
        s_ctx_tr, s_ctx_t, s_ctx_t_act = sem("ctx_transposed"), sem("ctx_t_ready"), sem("ctx_t_ready_act")
        s_kp, s_khi, s_klo = sem("k_product"), sem("k_hi_ready"), sem("k_lo_ready")
        s_kst = [sem(f"k_stack{b}_in") for b in range(BATCHES)]
        s_vp, s_vc, s_vt, s_ktail = sem("v_product"), sem("v_copied"), sem("v_tail_in"), sem("k_tail_ready")
        s_wsplit_hi, s_wsplit = sem("w_hi_ready"), sem("w_lo_ready")
        s_msk, s_cnt, s_mval = sem("mask_chain"), sem("mask_counts"), sem("mask_values")
        x_loaded, xt_ready, xh_done = sem("x_loaded"), sem("x_transposed"), sem("xt_hi_ready")
        gen_freed = sem("general_bank_freed")
        q_ready, qh_done = sem("q_product"), sem("q_hi_ready")
        stack_in = [sem("stack_a_in"), sem("stack_b_in")]
        s_ready, s_freed = sem("scores_ready"), sem("maxima_taken")
        split_hi, split_done = sem("max_hi_ready"), [sem("max_a_split"), sem("max_b_split")]
        aux_ready, aux_in = sem("maxima_transposed"), [sem("aux_a_in"), sem("aux_b_in")]
        st_ready, exp_done = sem("scores_t_ready"), sem("exp_done")
        pv_ready, recip_done, norm_done, att_done = sem("pv_ready"), sem("recip_done"), sem("normalised"), sem("attn_ready")
        at_ready, ah_done, al_done = sem("attn_transposed"), sem("at_hi_ready"), sem("at_lo_ready")
        o_ready, out_done = sem("out_product"), sem("out_ready")
        stored = sem("dram_stored")
        xr_loaded, xr_ready = sem("x_res_loaded"), sem("x_res_biased")

        STACK_PARTS = ((0, "hi"), (32, "lo"), (64, "hi"))
        K_PARTS = ((0, k_hi), (32, k_hi), (64, k_lo))
        N_STACK_DMAS = 4 * len(STACK_PARTS) + 1

        def k_bank(g):
            return bank[5 + g % 3]

        def v_bank(n):
            return bank[4 + n % 4]

        def column_group(w, g):
            return w.rearrange("(c p) n -> p c n", p=P)[:, :, P * g:P * (g + 1)]

        block = stack.enter_context(nc.Block())

        @block.sync
        def _(sp):
            sp.dma_start(ctx_main[:], ctx[:, 0:P, :].rearrange("b p c -> p b c")).then_inc(s_ctx, 16)
            sp.dma_start(ident[:], c_ident).then_inc(s_ident, 16)
            for b in range(BATCHES):
                sp.dma_start(ctx_rest[REM * b:REM * (b + 1), :], ctx[b, P:TEXT, :]).then_inc(s_ctx, 16)
                o = BATCHES * REM + IP * b
                sp.dma_start(ctx_rest[o:o + IP, :], ctx[b, TEXT:CTX, :]).then_inc(s_ctx, 16)
            sp.dma_start(small[0:8, 0:4], boxes.rearrange("b m c -> (b m) c")).then_inc(s_grid, 16)
            sp.dma_start(small[0:8, 8:8 + GRID_W + GRID_H], c_grid).then_inc(s_grid, 16)
            sp.dma_start(small[0:9, 128:128 + BATCHES * IP], c_pick).then_inc(s_grid, 16)
            sp.dma_start(row_raw[:], c_rows).then_inc(s_row_raw, 16)
            for g in range(GROUPS):
                cols = slice(P * g, P * (g + 1))
                sp.dma_start(w_kv[:, :, cols], column_group(wk, g)).then_inc(s_wk[g], 16)
                sp.dma_start(w_k_ip[:, :, cols], column_group(wk_ip, g)).then_inc(s_wk[g], 16)
            sp.dma_start(wq_raw[:], wq.rearrange("(c p) n -> p c n", p=P)).then_inc(s_wq, 16)
            sp.dma_start(x_in[:], x_rows[0:QB, :].rearrange("(a p) d -> p a d", p=P)).then_inc(x_loaded, 16)
            sp.wait_ge(s_row_consts, 1)
            for b in range(BATCHES):
                sp.dma_start(k_stack[b][ROW_MASK:STACK, :, :].bitcast(F32).rearrange("p (g j) k -> p g (j k)", j=4),
                             row_consts[:].bitcast(F32).unsqueeze(1).to_broadcast([STACK - ROW_MASK, GROUPS, 4 * CTX])
                             ).then_inc(s_rows, 16)
                sp.dma_start(v_tail[b][:], c_ones.unsqueeze(1).to_broadcast([P, GROUPS, 8 * VW])).then_inc(s_ones, 16)
            for g in range(GROUPS):
                sp.wait_ge(s_kp, g + 1)
                sp.dma_start(w_kv[:, :, P * g:P * (g + 1)], column_group(wv, g)).then_inc(s_wv, 16)
                if g in (1, 4):
                    b = 0 if g == 1 else 1
                    sp.wait_ge(s_mval, 4 * (b + 1))
                    sp.dma_start(mask_dram[:, b * SEQ:(b + 1) * SEQ], mask[:]).then_inc(stored, 16)

            sp.dma_start(w_v_ip, wv_ip.rearrange("(c p) n -> p c n", p=P)).then_inc(s_wv_ip, 16)

            def keys_to_stack(b):
                for row, src in K_PARTS:
                    for j in range(4):
                        sp.dma_start(k_stack[b][row:row + DH, j:HEADS:4, :].bitcast(F32),
                                     src[DH * j:DH * (j + 1), :, b, :].bitcast(F32)).then_inc(s_kst[b], 16)

            def rest_of_setup():
                sp.wait_ge(s_vp, 2)
                sp.dma_start(wo_raw[:, KC:2 * KC, :], wo.rearrange("(c p) n -> p c n", p=P)).then_inc(s_wo, 16)
                keys_to_stack(1)
                sp.wait_ge(s_ones, 16 * BATCHES)
                sp.wait_ge(s_vc, 4)
                for b in range(BATCHES):
                    for j in range(4):
                        r = 32 * j
                        sp.dma_start(v_tail[b][r:r + REM, :, VW * j:VW * j + DH],
                                     v_rest[REM * b:REM * (b + 1), :].rearrange("p (g j d) -> p g j d", j=4, d=DH)[:, :, j, :]
                                     ).then_inc(s_vt, 16)
                        sp.dma_start(v_tail[b][r + REM:r + TAIL, :, VW * (4 + j):VW * (4 + j) + DH],
                                     v_rest_ip[IP * b:IP * (b + 1), :].rearrange("p (g j d) -> p g j d", j=4, d=DH)[:, :, j, :]
                                     ).then_inc(s_vt, 16)
                sp.wait_ge(s_vp, len(V_UNITS))
                sp.dma_start(bias[:], b_out.rearrange("(a n) -> a n", a=1).to_broadcast([P, D])).then_inc(s_bias, 16)

            def body(it):
                t = it.t
                for n, groups in enumerate((SET_A, SET_B)):
                    if it.back:
                        sp.wait_ge(gen_freed, it.gen_after("AUX", n))
                        for i, g in enumerate(groups):
                            src = aux_rows[n][16 * i:16 * (i + 1), :].bitcast(F32).unsqueeze(1).to_broadcast([16, 4, QB])
                            sp.dma_start(q_stack[ROW_MAX:STACK, 4 * g:4 * g + 4, :].bitcast(F32), src
                                         ).then_inc(aux_in[n], 16)
                    if n == 0 and it.next:
                        sp.wait_ge(xt_ready, t * NX + NX)
                        sp.dma_start(x_in[:], x_rows[bass.ds(t * QB + QB, QB), :].rearrange("(a p) d -> p a d", p=P)
                                     ).then_inc(x_loaded, 16)
                if it.back:
                    sp.wait_ge(stored, t * 16 * QT)
                    sp.dma_start(x_res[:], x_rows[bass.ds(t * QB - QB, QB), :].rearrange("(a p) d -> p a d", p=P)
                                 ).then_inc(xr_loaded, 16)
                if not it.back:
                    sp.wait_ge(s_klo, 2 * GROUPS)
                    keys_to_stack(0)
                for n, groups in enumerate((SET_A, SET_B)):
                    g0, g1 = groups[0], groups[-1] + 1
                    if it.front:
                        sp.wait_ge(gen_freed, it.gen_after("Q", g1 - 1))
                        if it.back:
                            sp.wait_ge(st_ready, 15 * t - 15 + 3 * g1)
                        for row, part in STACK_PARTS:
                            src = q_hi if part == "hi" else q_lo
                            for j in range(4):
                                sp.dma_start(q_stack[row:row + DH, 4 * g0 + j:4 * g1:4, :].bitcast(F32),
                                             src[DH * j:DH * (j + 1), g0:g1, :].bitcast(F32)).then_inc(stack_in[n], 16)
                        src = mask_dram[:, bass.ds(t * QB, QB)].unsqueeze(1).to_broadcast([IP, 4 * len(groups), QB])
                        sp.dma_start(q_stack[ROW_MASK:ROW_MAX, 4 * g0:4 * g1, :].bitcast(F32), src
                                     ).then_inc(stack_in[n], 16)
                if not it.back:
                    rest_of_setup()
                if it.back:
                    for qt in range(QT):
                        sp.wait_ge(out_done, t * 4 - 4 + 2 * qt + 2)
                        sp.dma_start(out_rows[bass.ds(t * QB - QB + qt * P, P), :], out_sb[:, qt, :]).then_inc(stored, 16)

            iterations(sp, body)
            sp.wait_ge(stored, 16 * (BATCHES + QT * BLOCKS))

        @block.gpsimd
        def _(pool):
            nc.gpsimd.memset(inside, 1.0).then_inc(s_ones_row, 1)
            nc.gpsimd.memset(max_parts[0][:].bitcast(mybir.dt.uint32), 0).then_inc(s_fill, 1)
            for b in range(BATCHES):
                nc.gpsimd.memset(v_main[b][:], 1.0).then_inc(s_fill, 1)
            for b in range(BATCHES):
                pool.wait_ge(s_kst[b], 16 * 12)
            for b in range(BATCHES):
                nc.gpsimd.memset(k_tail[b][:].bitcast(mybir.dt.uint32), 0).then_inc(s_ktail_zero, 1)
            pool.wait_ge(s_wsplit_hi, 2)
            nc.gpsimd.tensor_tensor(wo_lo, wo_raw[:, KC:2 * KC, :], wo_hi.bitcast(F32), ALU.subtract).then_inc(s_wsplit, 1)
            pool.wait_ge(s_bias, 16)

            def body(it):
                t = it.t
                for stage, kind, args, gen, sc in it.steps():
                    if kind == "PV":
                        g, qt = args
                        if (g, qt) == (3, 0):
                            pool.wait_ge(xr_loaded, t * 16)
                            nc.gpsimd.tensor_tensor(x_res[:], x_res[:], bias[:].unsqueeze(1).to_broadcast([P, QT, D]),
                                                    ALU.add).then_inc(xr_ready, 1)
                        pool.wait_ge(norm_done, t * 10 - 10 + 2 * g + qt + 1)
                        nc.gpsimd.tensor_tensor(attn[:, qt, P * g:P * (g + 1)].rearrange("p (h d) -> p h d", d=DH),
                                                o_both[:, qt, 0:4, :], o_both[:, qt, 4:8, :], ALU.add
                                                ).then_inc(att_done, 1)

            iterations(pool, body)

        @block.scalar
        def _(act):
            for b in range(BATCHES):
                act.wait_ge(s_ctx_tr, 2 * b + 1)
                nc.scalar.activation(ctx_t[:, 0:4, b * TEXT:b * TEXT + P],
                                     bank[2 * b][:].rearrange("p (c k) -> p c k", c=4), ACT.Copy).then_inc(s_ctx_t_act, 1)
            for g in range(GROUPS):
                act.wait_ge(s_kp, g + 1)
                ps = k_bank(g)
                nc.scalar.activation(k_hi[:, g, :, 0:TEXT],
                                     ps[:, 0:BATCHES * TEXT].rearrange("p (b k) -> p b k", b=BATCHES),
                                     ACT.Copy, scale=SCALE).then_inc(s_khi, 1)
                nc.scalar.activation(k_hi[:, g, :, TEXT:CTX],
                                     ps[:, BATCHES * TEXT:BATCHES * CTX].rearrange("p (b k) -> p b k", b=BATCHES),
                                     ACT.Copy, scale=SCALE).then_inc(s_khi, 1)
                if g == 3:
                    act.wait_ge(s_wq, 16)
                    nc.scalar.activation(wq_hi[:], wq_raw[:], ACT.Copy).then_inc(s_wsplit_hi, 1)

            def copy_values(units):
                for n in units:
                    keys, c0, c1 = V_UNITS[n]
                    act.wait_ge(s_vp, n + 1)
                    src = v_bank(n)[:, 0:c1 - c0]
                    if keys in ("ip", "rest"):
                        dst = v_rest_ip if keys == "ip" else v_rest
                        nc.scalar.activation(dst[:, c0:c1], src[0:dst.shape[0], :], ACT.Copy).then_inc(s_vc, 1)
                    else:
                        b = 0 if keys == "batch 0" else 1
                        nc.scalar.activation(v_main[b][:, c0 // DH:c1 // DH, 0:DH], src.rearrange("p (h d) -> p h d", d=DH),
                                             ACT.Copy).then_inc(s_vc, 1)

            def x_high(u, count, ps):
                c0, c1 = X_CHUNKS[u]
                act.wait_ge(xt_ready, count)
                nc.scalar.activation(xt_hi[:, c0:c1, :].rearrange("p c q -> p (c q)"), ps[:, 0:(c1 - c0) * QB], ACT.Copy
                                     ).then_inc(xh_done, 1)

            for u in range(NX):
                x_high(u, u + 1, general[u % 2])

            def body(it):
                t = it.t
                if not it.back:
                    act.wait_ge(s_fill, 1 + BATCHES)
                    act.wait_ge(stored, 16 * BATCHES)
                    act.wait_ge(s_rows, 16 * BATCHES)
                for stage, kind, args, gen, sc in it.steps():
                    bank_a = general[(it.parity + gen) % 2]
                    if not it.back:
                        copy_values(V_PLACES.get((kind, *args), ()))
                        if (kind, *args) == W_O_PLACE:
                            act.wait_ge(s_wo, 16)
                            nc.scalar.activation(wo_hi, wo_raw[:, KC:2 * KC, :], ACT.Copy).then_inc(s_wsplit_hi, 1)
                    if kind == "X":
                        if args[0] == 0:
                            act.wait_ge(q_ready, t * GROUPS + GROUPS)
                        x_high(args[0], t * NX + NX + args[0] + 1, bank_a)
                    if kind == "Q":
                        g = args[0]
                        n = 0 if g in SET_A else 1
                        act.wait_ge(q_ready, t * GROUPS + g + 1)
                        if it.back:
                            act.wait_ge(stack_in[n], t * (16 * N_STACK_DMAS))
                        nc.scalar.activation(q_hi[:, g, :], bank_a[:, 0:QB], ACT.Copy).then_inc(qh_done, 1)
                    if kind == "ST":
                        g, u = args
                        act.wait_ge(st_ready, t * 15 - 15 + 3 * g + u + 1)
                        src = scores_t[(3 * g + u) % 2]
                        if u < 2:
                            dst = p_main[:, g % 2, 2 * u:2 * u + 2, :].rearrange("p h q -> p (h q)")
                            nc.scalar.activation(dst, src[:], ACT.Exp).then_inc(exp_done, 1)
                        else:
                            nc.scalar.activation(p_tail[:, g % 2, :], src[:, 0:QB], ACT.Exp).then_inc(exp_done, 1)
                    if kind == "AT":
                        qt = args[0]
                        for u, (c0, c1) in enumerate(AT_CHUNKS):
                            act.wait_ge(at_ready, t * 4 - 4 + 2 * qt + u + 1)
                            nc.scalar.activation(at_hi[:, qt, P * c0:P * c1], scores_t[u][:, 0:P * (c1 - c0)], ACT.Copy).then_inc(ah_done, 1)

                if not it.back:
                    copy_values(V_PLACES[None])

            iterations(act, body)

        @block.vector
        def _(dve):
            box, xs, ys = small[0:8, 0:4], small[0:8, 8:8 + GRID_W], small[0:8, 8 + GRID_W:8 + GRID_W + GRID_H]
            gx, gy = small[0:8, 144:144 + GRID_W], small[0:8, 208:208 + GRID_H]
            dve.wait_ge(s_grid, 48)
            nc.vector.tensor_copy(pick[0:9, :], small[0:9, 128:128 + BATCHES * IP])
            nc.vector.tensor_scalar(gx, xs, box[:, 0:1], None, ALU.is_ge)
            nc.vector.tensor_scalar(gy, ys, box[:, 1:2], None, ALU.is_ge).then_inc(s_msk, 1)
            dve.wait_ge(s_msk, 1)
            nc.vector.scalar_tensor_tensor(out=gx, in0=xs, scalar=box[:, 2:3], in1=gx, op0=ALU.is_le, op1=ALU.mult)
            nc.vector.scalar_tensor_tensor(out=gy, in0=ys, scalar=box[:, 3:4], in1=gy, op0=ALU.is_le, op1=ALU.mult
                                           ).then_inc(s_msk, 1)
            for b in range(BATCHES):
                dve.wait_ge(s_ctx_tr, 2 * b + 2)
                nc.vector.tensor_copy(ctx_t[:, 4:8, b * TEXT:b * TEXT + P],
                                      bank[2 * b + 1][:].rearrange("p (c k) -> p c k", c=4)).then_inc(s_ctx_t, 1)
            dve.wait_ge(s_ctx_tr, 5)
            rest = bank[4][:, 0:CC * BATCHES * TAIL].rearrange("p (c k) -> p c k", c=CC)
            nc.vector.tensor_copy(rest_t[:], rest)
            for b in range(BATCHES):
                nc.vector.tensor_copy(ctx_t[:, :, b * TEXT + P:(b + 1) * TEXT], rest[:, :, b * REM:(b + 1) * REM])
            nc.vector.tensor_copy(ctx_t[:, :, BATCHES * TEXT:], rest[:, :, BATCHES * REM:]).then_inc(s_ctx_t, 1)
            dve.wait_ge(s_ones_row, 1)
            dve.wait_ge(s_msk, 2)
            nc.vector.tensor_tensor(inside[0:8, :].rearrange("p (y x) -> p y x", x=GRID_W),
                                    gy.unsqueeze(2).to_broadcast([8, GRID_H, GRID_W]),
                                    gx.unsqueeze(1).to_broadcast([8, GRID_H, GRID_W]), ALU.mult).then_inc(s_msk, 1)
            dve.wait_ge(s_row_raw, 16)
            nc.vector.tensor_copy(row_consts[:], row_raw[:]).then_inc(s_row_consts, 1)
            def mask_values(first, end):
                for n in range(first, end):
                    dve.wait_ge(s_cnt, n + 1)
                    if n == 4:
                        dve.wait_ge(stored, 16)
                    c = n % 4
                    nc.vector.tensor_scalar(mask[:, 512 * c:512 * (c + 1)], bank[2 + n % 3][0:IP, :], -1.0, -NEG,
                                            ALU.max, ALU.mult).then_inc(s_mval, 1)

            for g in range(GROUPS):
                ps = k_bank(g)
                dve.wait_ge(s_khi, 2 * g + 2)
                for u, (c0, c1, k0, k1) in enumerate(((0, BATCHES * TEXT, 0, TEXT),
                                                      (BATCHES * TEXT, BATCHES * CTX, TEXT, CTX))):
                    for b in range(BATCHES):
                        w = (c1 - c0) // BATCHES
                        last = nc.vector.scalar_tensor_tensor(
                            out=k_lo[:, g, b, k0:k1], in0=ps[:, c0 + b * w:c0 + (b + 1) * w], scalar=SCALE,
                            in1=k_hi[:, g, b, k0:k1].bitcast(F32), op0=ALU.mult, op1=ALU.subtract)
                    last.then_inc(s_klo, 1)
                if g in COUNTS:
                    mask_values(*COUNTS[g])
                if g == 3:
                    dve.wait_ge(s_wsplit_hi, 1)
                    nc.vector.tensor_tensor(wq_lo[:], wq_raw[:], wq_hi[:].bitcast(F32), ALU.subtract
                                            ).then_inc(s_wsplit, 1)

            def rest_of_setup():
                dve.wait_ge(s_ktail_zero, BATCHES)
                dve.wait_ge(s_rows, 16 * BATCHES)
                for b in range(BATCHES):
                    for j in range(4):
                        nc.vector.tensor_copy(k_tail[b][0:STACK, j:HEADS:4, 32 * j:32 * j + TAIL],
                                              k_stack[b][0:STACK, j:HEADS:4, P:CTX].bitcast(F32)).then_inc(s_ktail, 1)

            def x_low(u, count, ps):
                c0, c1 = X_CHUNKS[u]
                dve.wait_ge(xh_done, count)
                nc.vector.tensor_tensor(xt_lo[:, c0:c1, :].rearrange("p c q -> p (c q)"), ps[:, 0:(c1 - c0) * QB],
                                        xt_hi[:, c0:c1, :].bitcast(F32).rearrange("p c q -> p (c q)"),
                                        ALU.subtract).then_inc(gen_freed, 1)

            for u in range(NX):
                x_low(u, u + 1, general[u % 2])

            def body(it):
                t = it.t
                if not it.back:
                    dve.wait_ge(s_fill, 1 + BATCHES)
                for stage, kind, args, gen, sc in it.steps():
                    bank_a = general[(it.parity + gen) % 2]
                    if kind == "X":
                        x_low(args[0], t * NX + NX + args[0] + 1, bank_a)
                    if kind == "Q":
                        g = args[0]
                        dve.wait_ge(qh_done, t * GROUPS + g + 1)
                        nc.vector.tensor_tensor(q_lo[:, g, :], bank_a[:, 0:QB], q_hi[:, g, :].bitcast(F32),
                                                ALU.subtract).then_inc(gen_freed, 1)
                    if kind == "S":
                        g, qt = args
                        for pair in range(2):
                            dve.wait_ge(s_ready, it.sc0 + sc + pair + 1)
                            src = scores[(sc + pair) % 2][:, 0:2 * CTX].rearrange("p (h k) -> p h k", h=2)
                            dst = neg_max[:, qt, g, 4 * pair:4 * pair + 4].rearrange("p (h s) -> p h s", s=2)
                            nc.vector.tensor_reduce(dst[:, :, 0], src[:, :, 0:TEXT], AX_X, ALU.max, negate=True)
                            nc.vector.tensor_reduce(dst[:, :, 1], src[:, :, TEXT:CTX], AX_X, ALU.max, negate=True
                                                    ).then_inc(s_freed, 1)
                        for n, groups in enumerate((SET_A, SET_B)):
                            if (g, qt) == (groups[-1], QT - 1):
                                c0, c1 = 8 * groups[0], 8 * (groups[-1] + 1)
                                parts = max_parts[n][:, :, 0:2 * (c1 - c0)].rearrange("p a (m e) -> p a m e", e=2)
                                whole = neg_max[:].rearrange("p a g e -> p a (g e)")[:, :, c0:c1]
                                dve.wait_ge(s_freed, it.sc0 + sc + 2)
                                nc.vector.tensor_copy(parts[:, :, :, 0], whole).then_inc(split_hi, 1)
                                dve.wait_ge(split_hi, t * 2 + (1 if n == 0 else 0))
                                nc.vector.tensor_tensor(parts[:, :, :, 1], whole, parts[:, :, :, 0].bitcast(F32),
                                                        ALU.subtract).then_inc(split_done[n], 1)
                    if kind == "AUX":
                        n = args[0]
                        dve.wait_ge(aux_ready, t * 2 - 2 + n + 1)
                        nc.vector.tensor_copy(aux_rows[n][:], bank_a[0:aux_rows[n].shape[0], 0:QB]
                                              ).then_inc(gen_freed, 1)
                    if kind == "PV":
                        g, qt = args
                        n = t * 10 - 10 + 2 * g + qt
                        dve.wait_ge(pv_ready, n + 1)
                        both = product[qt][:, 0:8 * VW].rearrange("p (e d) -> p e d", d=VW)
                        nc.vector.reciprocal(inv_den[:, qt, :], both[:, :, DH]).then_inc(recip_done, 1)
                        dve.wait_ge(recip_done, n + 1)
                        if g > 0:
                            dve.wait_ge(att_done, n - 1)
                        nc.vector.tensor_tensor(o_both[:, qt, :, :], both[:, :, 0:DH],
                                                inv_den[:, qt, :].unsqueeze(2).to_broadcast([P, 8, DH]), ALU.mult
                                                ).then_inc(norm_done, 1)
                    if kind == "AT":
                        qt = args[0]
                        for u, (c0, c1) in enumerate(AT_CHUNKS):
                            dve.wait_ge(ah_done, t * 4 - 4 + 2 * qt + u + 1)
                            nc.vector.tensor_tensor(at_lo[:, qt, P * c0:P * c1], scores_t[u][:, 0:P * (c1 - c0)],
                                                    at_hi[:, qt, P * c0:P * c1].bitcast(F32), ALU.subtract
                                                    ).then_inc(al_done, 1)
                    if kind == "O":
                        qt, half = args
                        if (qt, half) == (0, 0):
                            dve.wait_ge(xr_ready, t + 0)
                        dve.wait_ge(o_ready, t * 4 - 4 + 2 * qt + half + 1)
                        cols = slice(HALF * half, HALF * (half + 1))
                        nc.vector.tensor_tensor(out_sb[:, qt, cols], product[half][:, 0:HALF], x_res[:, qt, cols], ALU.add
                                                ).then_inc(out_done, 1)

                if not it.back:
                    rest_of_setup()

            iterations(dve, body)

        @block.tensor
        def _(pe):
            pe.wait_ge(s_ident, 16)
            pe.wait_ge(s_ctx, 16 * 5)
            for b in range(BATCHES):
                for half in range(2):
                    for c in range(4):
                        last = nc.tensor.transpose(bank[2 * b + half][:, P * c:P * (c + 1)],
                                                   ctx_main[:, b, P * (4 * half + c):P * (4 * half + c + 1)], ident[:])
                    last.then_inc(s_ctx_tr, 1)
            n = BATCHES * TAIL
            for c in range(CC):
                last = nc.tensor.transpose(bank[4][:, n * c:n * (c + 1)], ctx_rest[0:n, P * c:P * (c + 1)], ident[0:n, 0:n])
            last.then_inc(s_ctx_tr, 1)
            pe.wait_ge(s_ctx_t, BATCHES + 1)
            pe.wait_ge(s_ctx_t_act, BATCHES)
            text, both = BATCHES * TEXT, BATCHES * CTX
            for g in range(GROUPS):
                pe.wait_ge(s_wk[g], 32)
                if g >= 3:
                    pe.wait_ge(s_klo, 2 * (g - 2))
                ps = k_bank(g)
                for c in range(CC):
                    nc.tensor.matmul(ps[:, 0:text], w_kv[:, c, P * g:P * (g + 1)], ctx_t[:, c, 0:text],
                                     start=(c == 0), stop=(c == CC - 1))
                for c in range(CC):
                    last = nc.tensor.matmul(ps[:, text:both], w_k_ip[:, c, P * g:P * (g + 1)], ctx_t[:, c, text:both],
                                            start=(c == 0), stop=(c == CC - 1))
                last.then_inc(s_kp, 1)
                for n in range(*COUNTS.get(g, (0, 0))):
                    if n == 0:
                        pe.wait_ge(s_msk, 3)
                    b, c = n // 4, n % 4
                    if n >= 3:
                        pe.wait_ge(s_mval, n - 2)
                    nc.tensor.matmul(bank[2 + n % 3][0:IP, :], pick[0:9, IP * b:IP * (b + 1)],
                                     inside[:, 512 * c:512 * (c + 1)], start=True, stop=True).then_inc(s_cnt, 1)

            def make_values(units):
                for n in units:
                    keys, c0, c1 = V_UNITS[n]
                    if n == 0:
                        pe.wait_ge(s_klo, 2 * GROUPS)
                        pe.wait_ge(s_mval, 2 * 4)
                        pe.wait_ge(s_wv_ip, 16)
                    if n == 2:
                        pe.wait_ge(s_wv, 16 * GROUPS)
                    if n >= 4:
                        pe.wait_ge(s_vc, n - 3)
                    rows = {"ip": rest_t[:, :, BATCHES * REM:], "rest": rest_t[:, :, 0:BATCHES * REM],
                            "batch 0": ctx_t[:, :, 0:P], "batch 1": ctx_t[:, :, TEXT:TEXT + P]}[keys]
                    for c in range(CC):
                        last = nc.tensor.matmul(v_bank(n)[0:rows.shape[2], 0:c1 - c0], rows[:, c, :],
                                                (w_v_ip if keys == "ip" else w_kv)[:, c, c0:c1],
                                                start=(c == 0), stop=(c == CC - 1))
                    last.then_inc(s_vp, 1)

            def transpose_x(u, ps):
                c0, c1 = X_CHUNKS[u]
                for c in range(c0, c1):
                    for qt in range(QT):
                        at = (c - c0) * QB + qt * P
                        last = nc.tensor.transpose(ps[:, at:at + P], x_in[:, qt, P * c:P * (c + 1)], ident[:])
                last.then_inc(xt_ready, 1)

            pe.wait_ge(x_loaded, 16)
            for u in range(NX):
                if u >= 2:
                    pe.wait_ge(gen_freed, u - 1)
                transpose_x(u, general[u % 2])

            def free_general(it, gen):
                pe.wait_ge(gen_freed, it.gen0 + gen - 1)

            def split_product(ps, lhs_hi, lhs_lo, rhs_hi, rhs_lo):
                terms = [(l, r, c) for c in range(KC) for l, r in ((lhs_hi, rhs_hi), (lhs_lo, rhs_hi), (lhs_hi, rhs_lo))]
                for i, (l, r, c) in enumerate(terms):
                    last = nc.tensor.matmul(ps, l(c), r(c), start=(i == 0), stop=(i == len(terms) - 1))
                return last

            def body(it):
                t = it.t
                if not it.back:
                    pe.wait_ge(s_wsplit, 1)
                for stage, kind, args, gen, sc in it.steps():
                    if not it.back:
                        make_values(V_PLACES.get((kind, *args), ()))
                        if (kind, *args) == ("S", 0, 0):
                            pe.wait_ge(s_kst[0], 16 * 12)
                            pe.wait_ge(s_rows, 16 * BATCHES)
                    batch = it.batch[stage]
                    bank_a = general[(it.parity + gen) % 2]
                    if kind == "X":
                        if args[0] == 0:
                            pe.wait_ge(x_loaded, t * 16 + 32)
                        free_general(it, gen)
                        transpose_x(args[0], bank_a)
                    if kind == "Q":
                        g = args[0]
                        if g == 0:
                            pe.wait_ge(gen_freed, it.gen0 + 0)
                        free_general(it, gen)
                        cols = slice(P * g, P * (g + 1))
                        split_product(bank_a[:, 0:QB],
                                      lambda c: wq_hi[:, c, cols], lambda c: wq_lo[:, c, cols],
                                      lambda c: xt_hi[:, c, :], lambda c: xt_lo[:, c, :]).then_inc(q_ready, 1)
                    if kind == "S":
                        g, qt = args
                        if qt == 0 and g in (SET_A[0], SET_B[0]):
                            n = 0 if g in SET_A else 1
                            blocks = t + 1 if stage == FRONT else t + 0
                            pe.wait_ge(stack_in[n], blocks * (16 * N_STACK_DMAS))
                        for pair in range(2):
                            if it.back or sc + pair >= 2:
                                pe.wait_ge(s_freed, it.sc0 + sc + pair - 1)
                            for i in range(2):
                                h = 4 * g + 2 * pair + i
                                last = nc.tensor.matmul(scores[(sc + pair) % 2][:, i * CTX:(i + 1) * CTX],
                                                        q_stack[0:ROW_MAX, h, P * qt:P * (qt + 1)],
                                                        k_stack[batch][0:ROW_MAX, h, :], start=True, stop=True)
                            last.then_inc(s_ready, 1)
                    if kind == "AUX":
                        n = args[0]
                        pe.wait_ge(split_done[n], t + 0)
                        free_general(it, gen)
                        for qt in range(QT):
                            last = nc.tensor.transpose(bank_a[0:max_cols[n], P * qt:P * (qt + 1)],
                                                       max_parts[n][:, qt, :].bitcast(F32), ident[:])
                        last.then_inc(aux_ready, 1)
                    if kind == "ST":
                        g, u = args
                        if u == 0 and g in (SET_A[0], SET_B[0]):
                            n = 0 if g in SET_A else 1
                            pe.wait_ge(aux_in[n], t * (16 * len((SET_A, SET_B)[n])))
                        if g or u > 1:
                            pe.wait_ge(exp_done, t * 15 - 15 + 3 * g + u - 1)
                        ps = scores_t[(3 * g + u) % 2]
                        if u < 2:
                            for i in range(2):
                                h = 4 * g + 2 * u + i
                                last = nc.tensor.matmul(ps[:, QB * i:QB * (i + 1)], k_stack[batch][0:STACK, h, 0:P],
                                                        q_stack[0:STACK, h, :], start=True, stop=True)
                        else:
                            for i in range(4):
                                h = 4 * g + i
                                last = nc.tensor.matmul(ps[:, 0:QB], k_tail[batch][0:STACK, h, :],
                                                        q_stack[0:STACK, h, :], start=(i == 0), stop=(i == 3))
                        last.then_inc(st_ready, 1)
                    if kind == "PV":
                        g, qt = args
                        if qt == 0:
                            pe.wait_ge(exp_done, t * 15 - 15 + 3 * g + 3)
                        if g > 0:
                            pe.wait_ge(norm_done, t * 10 - 10 + 2 * g + qt - 1)
                        queries = slice(P * qt, P * (qt + 1))
                        nc.tensor.matmul(product[qt][:, 0:8 * VW], p_tail[:, g % 2, queries], v_tail[batch][:, g, :],
                                         start=True, stop=False)
                        for j in range(4):
                            last = nc.tensor.matmul(product[qt][:, VW * j:VW * (j + 1)], p_main[:, g % 2, j, queries],
                                                    v_main[batch][:, 4 * g + j, :], start=False, stop=(j == 3))
                        last.then_inc(pv_ready, 1)
                    if kind == "AT":
                        qt = args[0]
                        pe.wait_ge(att_done, t * 10 - 1 + qt)
                        for u, (c0, c1) in enumerate(AT_CHUNKS):
                            if qt > 0:
                                pe.wait_ge(al_done, t * 4 - 4 + 2 * qt + u - 1)
                            for c in range(c0, c1):
                                last = nc.tensor.transpose(scores_t[u][:, P * (c - c0):P * (c - c0 + 1)],
                                                           attn[:, qt, P * c:P * (c + 1)], ident[:])
                            last.then_inc(at_ready, 1)
                    if kind == "O":
                        qt, half = args
                        if half == 0:
                            pe.wait_ge(al_done, t * 4 - 4 + 2 * qt + 2)
                        if qt > 0:
                            pe.wait_ge(out_done, t * 4 - 4 + 2 * qt + half - 1)
                        cols = slice(HALF * half, HALF * (half + 1))
                        split_product(product[half][:, 0:HALF],
                                      lambda c: at_hi[:, qt, P * c:P * (c + 1)], lambda c: at_lo[:, qt, P * c:P * (c + 1)],
                                      lambda c: wo_hi[:, c, cols], lambda c: wo_lo[:, c, cols]).then_inc(o_ready, 1)

                if not it.back:
                    make_values(V_PLACES[None])
                    pe.wait_ge(s_vc, len(V_UNITS))
                    pe.wait_ge(s_ktail, 4 * BATCHES)
                    pe.wait_ge(s_vt, 16 * 8 * BATCHES)
                    pe.wait_ge(s_wsplit, 2)

            iterations(pe, body)


_INS = ["x", "ctx_2048", "fside_Bx4x4_0", "L0_xattn_w_q", "L0_xattn_w_k", "L0_xattn_w_v",
        "L0_xattn_w_k_ip", "L0_xattn_w_v_ip", "L0_xattn_w_out", "L0_xattn_b_out"]


def shape_constants():
    grid = np.zeros((8, GRID_W + GRID_H), np.float32)
    grid[:, :GRID_W] = np.linspace(0.0, 1.0, GRID_W, dtype=np.float32)
    grid[:, GRID_W:] = np.linspace(0.0, 1.0, GRID_H, dtype=np.float32)
    rows = np.zeros((STACK - ROW_MASK, 4, CTX), np.float32)
    for r in range(IP):
        rows[r, :, TEXT + r] = 1.0
    for j in range(4):
        rows[IP + 4 * j:IP + 4 * j + 2, j, :TEXT] = 1.0
        rows[IP + 4 * j + 2:IP + 4 * j + 4, j, TEXT:] = 1.0
    ones = np.zeros((P, 8, VW), np.float32)
    for j in range(4):
        ones[32 * j:32 * j + REM, j, DH] = 1.0
        ones[32 * j + REM:32 * j + TAIL, 4 + j, DH] = 1.0
    pick = np.zeros((9, BATCHES, IP), np.float32)
    for b in range(BATCHES):
        for m in range(4):
            pick[4 * b + m, b, :DUMMIES] = -1.0
            pick[4 * b + m, b, DUMMIES + m] = 1.0
        pick[8, b, DUMMIES:] = -1.0
    return {"identity": np.eye(P, dtype=np.float32), "grid": grid, "stack_rows": rows.reshape(STACK - ROW_MASK, -1),
            "tail_ones": ones.reshape(P, -1), "mask_pick": pick.reshape(9, -1)}


def kernel(**inputs):
    import concourse.bacc as bacc
    from concourse.bass_utils import run_bass_kernel_spmd

    nc = bacc.Bacc("TRN2", target_bir_lowering=False, num_devices=1)
    arrays = {f"in_{name}": np.ascontiguousarray(inputs[name]) for name in _INS}
    arrays |= {f"const_{name}": a for name, a in shape_constants().items()}
    args = [nc.dram_tensor(name, a.shape, mybir.dt.from_np(a.dtype), kind="ExternalInput").ap()
            for name, a in arrays.items()]
    out = nc.dram_tensor("out_0", (BATCHES, SEQ, D), F32, kind="ExternalOutput").ap()
    attention_kernel(nc, *args, out)
    r = run_bass_kernel_spmd(nc, [arrays], core_ids=[0])
    return r.results[0]["out_0"]
```

```python
from contextlib import ExitStack

import numpy as np

import concourse.bass as bass
from concourse import mybir

F32 = mybir.dt.float32
F32R = mybir.dt.float32r
BF16 = mybir.dt.bfloat16
F16 = mybir.dt.float16
ALU = mybir.AluOpType
ACT = mybir.ActivationFunctionType
AX_X = mybir.AxisListType.X

P = 128
BATCHES, SEQ, D = 2, 2048, 640
CTX, CTX_D = 154, 1024
HEADS, DH = 20, 32
IP = 8
DUMMIES = 4
TEXT = CTX - IP
REM = TEXT - P
TAIL = REM + IP
NEG = -10000.0
SCALE = float(np.float32(1.0) / np.sqrt(np.float32(DH)))

KC = D // P
CC = CTX_D // P
GROUPS = HEADS // 4
QB = 256
QT = QB // P
BLOCKS = BATCHES * SEQ // QB
PER_BATCH = BLOCKS // BATCHES
VW = DH + 1
V_PARTS = 3
VB = VW + DH
VALUES = VB + DH
P_SLOTS = 3
HALF = D // 2
ROW_MASK, ROW_MAX = 96, 104
STACK = 120
GRID_W, GRID_H = 64, 32
SET_A, SET_B = (0, 1, 2), (3, 4)

FRONT, BACK, NEXT = "front", "back", "next"
STEPS = [
    (BACK, "AUX", 0), (BACK, "S", 3, 0), (FRONT, "Q", 0), (BACK, "S", 3, 1), (FRONT, "Q", 1), (BACK, "S", 4, 0),
    (BACK, "ST", 0, 0), (BACK, "ST", 0, 1), (BACK, "S", 4, 1), (FRONT, "Q", 2), (BACK, "ST", 0, 2), (BACK, "ST", 1, 0),
    (BACK, "AUX", 1), (BACK, "ST", 1, 1), (FRONT, "Q", 3), (BACK, "PV", 0, 0), (BACK, "ST", 1, 2), (BACK, "ST", 2, 0),
    (BACK, "PV", 0, 1), (BACK, "ST", 2, 1), (BACK, "PV", 1, 0), (BACK, "ST", 2, 2), (BACK, "ST", 3, 0),
    (BACK, "PV", 1, 1), (BACK, "ST", 3, 1), (BACK, "PV", 2, 0), (BACK, "ST", 3, 2), (BACK, "PV", 2, 1),
    (BACK, "ST", 4, 0), (FRONT, "Q", 4), (BACK, "ST", 4, 1), (BACK, "ST", 4, 2), (BACK, "PV", 3, 0), (BACK, "PV", 3, 1),
    (NEXT, "X", 0), (BACK, "PV", 4, 0), (BACK, "PV", 4, 1), (FRONT, "S", 0, 0), (BACK, "AT", 0, 0), (BACK, "AT", 0, 1),
    (NEXT, "X", 1), (NEXT, "X", 2), (FRONT, "S", 0, 1), (BACK, "AT", 1, 0), (BACK, "AT", 1, 1), (BACK, "O", 0, 0),
    (FRONT, "S", 1, 0), (BACK, "O", 0, 1), (FRONT, "S", 1, 1), (BACK, "O", 1, 0), (FRONT, "S", 2, 0), (FRONT, "S", 2, 1),
    (BACK, "O", 1, 1),
]
X_CHUNKS = ((0, 2), (2, 4), (4, 5))
NX = len(X_CHUNKS)
AT_CHUNKS = ((0, 4), (4, 5))

V_UNITS = [(keys, c0, c1) for keys in ("ip", "rest", "batch 0", "batch 1") for c0, c1 in ((0, 512), (512, D))]
V_PLACES = {("X", 0): (0, 1), ("S", 1, 0): (2, 3), ("S", 2, 0): (4, 5), None: (6, 7)}
W_O_PLACE = ("S", 2, 0)
COUNTS = {0: (0, 3), 1: (3, 4), 3: (4, 7), 4: (7, 8)}
GENERAL = {"X": 1, "AUX": 1, "Q": 1}
SCORES = {"S": 2}


def uses(stage, table):
    return sum(table.get(s[1], 0) for s in STEPS if s[0] == stage)


GEN_F, GEN_B, GEN_N = (uses(stage, GENERAL) for stage in (FRONT, BACK, NEXT))
SC_F, SC_B = uses(FRONT, SCORES), uses(BACK, SCORES)
GEN_ALL = GEN_F + GEN_B + GEN_N


class Iteration:

    def __init__(self, t, stages, front_batch, back_batch):
        self.t, self.stages = t, stages
        self.front, self.back, self.next = (stage in stages for stage in (FRONT, BACK, NEXT))
        self.batch = {FRONT: front_batch, BACK: back_batch, NEXT: None}
        if isinstance(t, int) and t == 0:
            self.gen0, self.sc0 = GEN_N, 0
        else:
            self.gen0, self.sc0 = t * GEN_ALL + (GEN_N - GEN_B), t * (SC_F + SC_B) - SC_B
            if isinstance(t, int) and t == BLOCKS:
                self.gen0 -= GEN_N
        self.parity = (self.gen0 if isinstance(t, int) else GEN_N - GEN_B) % 2

    def steps(self, late=None):
        gen = sc = 0
        steps = []
        for stage, kind, *args in STEPS:
            if stage in self.stages:
                steps.append((stage, kind, args, gen, sc))
                gen += GENERAL.get(kind, 0)
                sc += SCORES.get(kind, 0)
        if late:
            places = [i + 0.5 + late[1] if step[1] == late[0] else i for i, step in enumerate(steps)]
            steps = [steps[i] for i in sorted(range(len(steps)), key=lambda i: places[i])]
        return steps

    def gen_after(self, kind, *args, use=0):
        for _, k, a, gen, _ in self.steps():
            if k == kind and tuple(a) == args:
                return self.gen0 + gen + use + 1


def iterations(engine, body):
    body(Iteration(0, (FRONT, NEXT), 0, 0))
    with engine.Fori(1, PER_BATCH) as t:
        body(Iteration(t, (FRONT, BACK, NEXT), 0, 0))
    body(Iteration(PER_BATCH, (FRONT, BACK, NEXT), 1, 0))
    with engine.Fori(PER_BATCH + 1, BLOCKS - 1) as t:
        body(Iteration(t, (FRONT, BACK, NEXT), 1, 1))
    body(Iteration(BLOCKS - 1, (FRONT, BACK), 1, 1))
    body(Iteration(BLOCKS, (BACK,), 1, 1))


def attention_kernel(nc, x, ctx, boxes, wq, wk, wv, wk_ip, wv_ip, wo, b_out,
                     c_ident, c_grid, c_rows, c_ones, c_pick, out):
    x_rows = x.rearrange("b s d -> (b s) d")
    out_rows = out.rearrange("b s d -> (b s) d")
    mask_dram = nc.dram_tensor("mask_scratch", (IP, BATCHES * SEQ), F32, kind="Internal").ap()

    with ExitStack() as stack:
        def sb(name, shape, dt=F32, where=stack):
            return where.enter_context(nc.sbuf_tensor(name, shape, dt))

        def sem(name):
            return stack.enter_context(nc.semaphore(name))

        ident = sb("ident", [P, P])
        with ExitStack() as setup:
            wq_raw, wo_raw = sb("wq_raw", [P, KC, D], where=setup), sb("wo_raw", [P, 2 * KC, D], where=setup)
        wq_lo = sb("wq_lo", [P, KC, D], F32R)
        wo_both = sb("wo_both", [P, 2 * KC, D], F32R)
        wo_hi, wo_lo = wo_both[:, 0:KC, :], wo_both[:, KC:2 * KC, :]
        wq_hi = sb("wq_hi", [P, KC, D], F32R)
        k_stack = [sb(f"k_stack{b}", [P, HEADS, CTX], F32R) for b in range(BATCHES)]
        k_tail = [sb(f"k_tail{b}", [P, HEADS, P], F32R) for b in range(BATCHES)]
        v_main = [sb(f"v_main{b}", [P, HEADS, VALUES], BF16) for b in range(BATCHES)]
        v_tail = [sb(f"v_tail{b}", [P, GROUPS, 8 * VW]) for b in range(BATCHES)]
        max_cols = [80, 16 * len(SET_B)]
        max_parts = [sb("max_parts_a", [P, QT, max_cols[0]], F32R), sb("max_parts_b", [P, QT, max_cols[1]], F32R)]
        neg_max = sb("neg_max", [P, QT, GROUPS, 8])
        x_in = sb("x_in", [P, QT, D])

        with ExitStack() as setup:
            ctx_main = sb("ctx_main", [P, BATCHES, CTX_D], where=setup)
            ctx_rest = sb("ctx_rest", [P, CTX_D], where=setup)
            mask = sb("mask", [IP, SEQ], where=setup)
            w_k_ip = sb("w_k_ip", [P, CC, D], where=setup)
            w_kv = sb("w_kv", [P, CC, D], where=setup)
            ctx_t = sb("ctx_t", [P, CC, BATCHES * CTX], where=setup)
            rest_t = sb("rest_t", [P, CC, BATCHES * TAIL], where=setup)
            small = sb("small", [16, 256], where=setup)
            pick = sb("pick", [16, BATCHES * IP], BF16, setup)
            with ExitStack() as first:
                row_raw = sb("row_raw", [STACK - ROW_MASK, 4 * CTX], where=first)
                row_consts = sb("row_consts", [STACK - ROW_MASK, 4 * CTX], F32R, first)
            v_rest = sb("v_rest", [BATCHES * REM, D], where=setup)
            v_rest_ip = sb("v_rest_ip", [BATCHES * IP, D], where=setup)
            v_left = sb("v_left", [P, 512], where=setup)
        w_v_ip = wo_raw[:, 0:CC, :]
        inside = wo_raw[0:9, CC:2 * KC, :].bitcast(BF16).rearrange("p a b -> p (a b)")[:, 0:SEQ]
        k_hi, k_lo = (k_tail[i][:].rearrange("p h k -> p (h k)")[:, 0:GROUPS * BATCHES * CTX]
                      .rearrange("p (g b k) -> p g b k", g=GROUPS, b=BATCHES) for i in range(2))

        xt_hi, xt_lo = sb("xt_hi", [P, KC, QB], F32R), sb("xt_lo", [P, KC, QB], F32R)
        q_hi, q_lo = sb("q_hi", [P, GROUPS, QB], F32R), sb("q_lo", [P, GROUPS, QB], F32R)
        q_stack = sb("q_stack", [P, HEADS, QB], F32R)
        aux_rows = [sb("aux_a", [16 * len(SET_A), QB], F32R), sb("aux_b", [16 * len(SET_B), QB], F32R)]
        p_lo = sb("p_lo", [P, P_SLOTS, 4, QB], F16)
        with ExitStack() as turns:
            at_hi_0, at_lo_0 = (sb(f"at_{part}_0", [P, QT, 4 * P], F32R, turns) for part in ("hi", "lo"))
            at_hi_1, at_lo_1 = (sb(f"at_{part}_1", [P, QT, P], F32R, turns) for part in ("hi", "lo"))
            at_hi, at_lo = (at_hi_0, at_hi_1), (at_lo_0, at_lo_1)
        p_whole = sb("p_whole", [P, 2, 2, QB])
        p_hi = sb("p_hi", [P, P_SLOTS, 4, QB], F16)
        p_tail = sb("p_tail", [P, P_SLOTS, QB])
        inv_den = sb("inv_den", [P, QT, 8])
        o_parts = sb("o_parts", [P, QT, 12, DH])
        attn = sb("attn", [P, QT, D])
        bias = sb("bias", [P, D])
        x_res = sb("x_res", [P, QT, D])
        out_sb = sb("out_sb", [P, QT, D])

        psum = stack.enter_context(nc.psum_tensor("psum", [P, 8 * 512], F32))
        bank = [psum[:, 512 * i:512 * (i + 1)] for i in range(8)]
        general, scores, product, scores_t = bank[0:2], bank[2:4], bank[4:6], bank[6:8]
        product_1 = [psum[:, 512 * (4 + qt):512 * (4 + qt) + 8 * VB].rearrange("p (e d) -> p e d", d=VB)[:, :, 0:VW]
                     for qt in range(QT)]
        product_2 = [bank[4 + qt][:, 0:4 * VB].rearrange("p (e d) -> p e d", d=VB)[:, :, VW:VB] for qt in range(QT)]

        s_ident, s_ctx, s_grid, s_rows = sem("ident_in"), sem("ctx_in"), sem("grid_in"), sem("stack_rows_in")
        s_ones_row = sem("ones_row_filled")
        s_row_raw, s_row_consts = sem("row_consts_in"), sem("row_consts_ready")
        s_wk = [sem(f"wk_in{g}") for g in range(GROUPS)]
        s_wv, s_wv_ip, s_wq, s_wo = sem("wv_in"), sem("wv_ip_in"), sem("wq_in"), sem("wo_in")
        s_ones, s_bias, s_fill, s_ktail_zero = sem("ones_in"), sem("bias_in"), sem("filled"), sem("k_tail_zero")
        s_ctx_tr, s_ctx_t, s_ctx_t_act = sem("ctx_transposed"), sem("ctx_t_ready"), sem("ctx_t_ready_act")
        s_kp, s_khi, s_klo = sem("k_product"), sem("k_hi_ready"), sem("k_lo_ready")
        s_kst = [sem(f"k_stack{b}_in") for b in range(BATCHES)]
        s_vp, s_vc, s_vt, s_ktail = sem("v_product"), sem("v_copied"), sem("v_tail_in"), sem("k_tail_ready")
        s_vsplit = sem("v_split")
        s_wsplit_hi, s_wsplit = sem("w_hi_ready"), sem("w_lo_ready")
        s_msk, s_cnt, s_mval = sem("mask_chain"), sem("mask_counts"), sem("mask_values")
        x_loaded, xt_ready, xh_done = sem("x_loaded"), sem("x_transposed"), sem("xt_hi_ready")
        gen_freed = sem("general_bank_freed")
        q_ready, qh_done = sem("q_product"), sem("q_hi_ready")
        stack_in = [sem("stack_a_in"), sem("stack_b_in")]
        s_ready, s_freed = sem("scores_ready"), sem("maxima_taken")
        split_hi, split_done = sem("max_hi_ready"), [sem("max_a_split"), sem("max_b_split")]
        aux_ready, aux_in = sem("maxima_transposed"), [sem("aux_a_in"), sem("aux_b_in")]
        norm_first = sem("first_part_normalised")
        p_split, att_half = sem("p_lo_ready"), sem("attn_half_ready")
        st_ready, exp_done = sem("scores_t_ready"), sem("exp_done")
        pv_ready, recip_done, norm_done, att_done = sem("pv_ready"), sem("recip_done"), sem("normalised"), sem("attn_ready")
        at_ready, ah_done, al_done = ([sem(f"{name}_{u}") for u in range(2)]
                                      for name in ("attn_transposed", "at_hi_ready", "at_lo_ready"))
        o_ready, out_done = sem("out_product"), sem("out_ready")
        stored = sem("dram_stored")
        xr_loaded, xr_ready = sem("x_res_loaded"), sem("x_res_biased")

        STACK_PARTS = ((0, "hi"), (32, "lo"), (64, "hi"))
        K_PARTS = ((0, k_hi), (32, k_hi), (64, k_lo))
        N_STACK_DMAS = 4 * len(STACK_PARTS) + 1

        def k_bank(g):
            return bank[5 + g % 3]

        def v_bank(n):
            return bank[4 + n % 4]

        def column_group(w, g):
            return w.rearrange("(c p) n -> p c n", p=P)[:, :, P * g:P * (g + 1)]

        block = stack.enter_context(nc.Block())

        @block.sync
        def _(sp):
            sp.dma_start(ctx_main[:], ctx[:, 0:P, :].rearrange("b p c -> p b c")).then_inc(s_ctx, 16)
            sp.dma_start(ident[:], c_ident).then_inc(s_ident, 16)
            for b in range(BATCHES):
                sp.dma_start(ctx_rest[REM * b:REM * (b + 1), :], ctx[b, P:TEXT, :]).then_inc(s_ctx, 16)
                o = BATCHES * REM + IP * b
                sp.dma_start(ctx_rest[o:o + IP, :], ctx[b, TEXT:CTX, :]).then_inc(s_ctx, 16)
            sp.dma_start(small[0:8, 0:4], boxes.rearrange("b m c -> (b m) c")).then_inc(s_grid, 16)
            sp.dma_start(small[0:8, 8:8 + GRID_W + GRID_H], c_grid).then_inc(s_grid, 16)
            sp.dma_start(small[0:9, 128:128 + BATCHES * IP], c_pick).then_inc(s_grid, 16)
            sp.dma_start(row_raw[:], c_rows).then_inc(s_row_raw, 16)
            for g in range(GROUPS):
                cols = slice(P * g, P * (g + 1))
                sp.dma_start(w_kv[:, :, cols], column_group(wk, g)).then_inc(s_wk[g], 16)
                sp.dma_start(w_k_ip[:, :, cols], column_group(wk_ip, g)).then_inc(s_wk[g], 16)
            sp.dma_start(wq_raw[:], wq.rearrange("(c p) n -> p c n", p=P)).then_inc(s_wq, 16)
            sp.dma_start(x_in[:], x_rows[0:QB, :].rearrange("(a p) d -> p a d", p=P)).then_inc(x_loaded, 16)
            sp.wait_ge(s_row_consts, 1)
            for b in range(BATCHES):
                sp.dma_start(k_stack[b][ROW_MASK:STACK, :, :].bitcast(F32).rearrange("p (g j) k -> p g (j k)", j=4),
                             row_consts[:].bitcast(F32).unsqueeze(1).to_broadcast([STACK - ROW_MASK, GROUPS, 4 * CTX])
                             ).then_inc(s_rows, 16)
                sp.dma_start(v_tail[b][:], c_ones.unsqueeze(1).to_broadcast([P, GROUPS, 8 * VW])).then_inc(s_ones, 16)
            for g in range(GROUPS):
                sp.wait_ge(s_kp, g + 1)
                sp.dma_start(w_kv[:, :, P * g:P * (g + 1)], column_group(wv, g)).then_inc(s_wv, 16)
                if g in (1, 4):
                    b = 0 if g == 1 else 1
                    sp.wait_ge(s_mval, 4 * (b + 1))
                    sp.dma_start(mask_dram[:, b * SEQ:(b + 1) * SEQ], mask[:]).then_inc(stored, 16)

            sp.dma_start(w_v_ip, wv_ip.rearrange("(c p) n -> p c n", p=P)).then_inc(s_wv_ip, 16)

            def keys_to_stack(b):
                for row, src in K_PARTS:
                    for j in range(4):
                        sp.dma_start(k_stack[b][row:row + DH, j:HEADS:4, :].bitcast(F32),
                                     src[DH * j:DH * (j + 1), :, b, :].bitcast(F32)).then_inc(s_kst[b], 16)

            def rest_of_setup():
                sp.wait_ge(s_vp, 2)
                sp.dma_start(wo_raw[:, KC:2 * KC, :], wo.rearrange("(c p) n -> p c n", p=P)).then_inc(s_wo, 16)
                keys_to_stack(1)
                sp.wait_ge(s_ones, 16 * BATCHES)
                sp.wait_ge(s_vc, 4)
                for b in range(BATCHES):
                    for j in range(4):
                        r = 32 * j
                        sp.dma_start(v_tail[b][r:r + REM, :, VW * j:VW * j + DH],
                                     v_rest[REM * b:REM * (b + 1), :].rearrange("p (g j d) -> p g j d", j=4, d=DH)[:, :, j, :]
                                     ).then_inc(s_vt, 16)
                        sp.dma_start(v_tail[b][r + REM:r + TAIL, :, VW * (4 + j):VW * (4 + j) + DH],
                                     v_rest_ip[IP * b:IP * (b + 1), :].rearrange("p (g j d) -> p g j d", j=4, d=DH)[:, :, j, :]
                                     ).then_inc(s_vt, 16)
                sp.wait_ge(s_vp, len(V_UNITS))
                sp.dma_start(bias[:], b_out.rearrange("(a n) -> a n", a=1).to_broadcast([P, D])).then_inc(s_bias, 16)

            def body(it):
                t = it.t
                for n, groups in enumerate((SET_A, SET_B)):
                    if it.back:
                        sp.wait_ge(gen_freed, it.gen_after("AUX", n))
                        for i, g in enumerate(groups):
                            src = aux_rows[n][16 * i:16 * (i + 1), :].bitcast(F32).unsqueeze(1).to_broadcast([16, 4, QB])
                            sp.dma_start(q_stack[ROW_MAX:STACK, 4 * g:4 * g + 4, :].bitcast(F32), src
                                         ).then_inc(aux_in[n], 16)
                    if n == 0 and it.next:
                        sp.wait_ge(xt_ready, t * NX + NX)
                        sp.dma_start(x_in[:], x_rows[bass.ds(t * QB + QB, QB), :].rearrange("(a p) d -> p a d", p=P)
                                     ).then_inc(x_loaded, 16)
                if it.back:
                    sp.wait_ge(stored, t * 16 * QT)
                    sp.dma_start(x_res[:], x_rows[bass.ds(t * QB - QB, QB), :].rearrange("(a p) d -> p a d", p=P)
                                 ).then_inc(xr_loaded, 16)
                if not it.back:
                    sp.wait_ge(s_klo, 2 * GROUPS)
                    keys_to_stack(0)
                for n, groups in enumerate((SET_A, SET_B)):
                    g0, g1 = groups[0], groups[-1] + 1
                    if it.front:
                        sp.wait_ge(gen_freed, it.gen_after("Q", g1 - 1))
                        if it.back:
                            sp.wait_ge(st_ready, 15 * t - 15 + 3 * g1)
                        for row, part in STACK_PARTS:
                            src = q_hi if part == "hi" else q_lo
                            for j in range(4):
                                sp.dma_start(q_stack[row:row + DH, 4 * g0 + j:4 * g1:4, :].bitcast(F32),
                                             src[DH * j:DH * (j + 1), g0:g1, :].bitcast(F32)).then_inc(stack_in[n], 16)
                        src = mask_dram[:, bass.ds(t * QB, QB)].unsqueeze(1).to_broadcast([IP, 4 * len(groups), QB])
                        sp.dma_start(q_stack[ROW_MASK:ROW_MAX, 4 * g0:4 * g1, :].bitcast(F32), src
                                     ).then_inc(stack_in[n], 16)
                if not it.back:
                    rest_of_setup()
                if it.back:
                    for qt in range(QT):
                        sp.wait_ge(out_done, t * 4 - 4 + 2 * qt + 2)
                        sp.dma_start(out_rows[bass.ds(t * QB - QB + qt * P, P), :], out_sb[:, qt, :]).then_inc(stored, 16)

            iterations(sp, body)
            sp.wait_ge(stored, 16 * (BATCHES + QT * BLOCKS))

        @block.gpsimd
        def _(pool):
            nc.gpsimd.memset(inside, 1.0).then_inc(s_ones_row, 1)
            nc.gpsimd.memset(max_parts[0][:].bitcast(mybir.dt.uint32), 0).then_inc(s_fill, 1)
            for b in range(BATCHES):
                nc.gpsimd.memset(v_main[b][:, :, DH:VW], 1.0).then_inc(s_fill, 1)
            for b in range(BATCHES):
                pool.wait_ge(s_kst[b], 16 * 12)
            for b in range(BATCHES):
                nc.gpsimd.memset(k_tail[b][:].bitcast(mybir.dt.uint32), 0).then_inc(s_ktail_zero, 1)
            pool.wait_ge(s_wsplit_hi, 2)
            nc.gpsimd.tensor_tensor(wo_lo, wo_raw[:, KC:2 * KC, :], wo_hi.bitcast(F32), ALU.subtract).then_inc(s_wsplit, 1)
            pool.wait_ge(s_bias, 16)

            def body(it):
                t = it.t
                for stage, kind, args, gen, sc in it.steps():
                    if kind == "PV":
                        g, qt = args
                        pool.wait_ge(norm_first, t * 10 - 10 + 2 * g + qt + 1)
                        cols = attn[:, qt, P * g:P * (g + 1)].rearrange("p (h d) -> p h d", d=DH)
                        nc.gpsimd.tensor_tensor(cols, o_parts[:, qt, 0:4, :], o_parts[:, qt, 4:8, :], ALU.add
                                                ).then_inc(att_half, 1)
                        pool.wait_ge(att_half, t * 10 - 10 + 2 * g + qt + 1)
                        pool.wait_ge(norm_done, t * 10 - 10 + 2 * g + qt + 1)
                        nc.gpsimd.tensor_tensor(cols, cols, o_parts[:, qt, 8:12, :], ALU.add).then_inc(att_done, 1)
                        if (g, qt) == (GROUPS - 1, QT - 1):
                            pool.wait_ge(xr_loaded, t * 16)
                            nc.gpsimd.tensor_tensor(x_res[:], x_res[:], bias[:].unsqueeze(1).to_broadcast([P, QT, D]),
                                                    ALU.add).then_inc(xr_ready, 1)

            iterations(pool, body)

        @block.scalar
        def _(act):
            for b in range(BATCHES):
                act.wait_ge(s_ctx_tr, 2 * b + 1)
                nc.scalar.activation(ctx_t[:, 0:4, b * TEXT:b * TEXT + P],
                                     bank[2 * b][:].rearrange("p (c k) -> p c k", c=4), ACT.Copy).then_inc(s_ctx_t_act, 1)
            for g in range(GROUPS):
                act.wait_ge(s_kp, g + 1)
                ps = k_bank(g)
                nc.scalar.activation(k_hi[:, g, :, 0:TEXT],
                                     ps[:, 0:BATCHES * TEXT].rearrange("p (b k) -> p b k", b=BATCHES),
                                     ACT.Copy, scale=SCALE).then_inc(s_khi, 1)
                nc.scalar.activation(k_hi[:, g, :, TEXT:CTX],
                                     ps[:, BATCHES * TEXT:BATCHES * CTX].rearrange("p (b k) -> p b k", b=BATCHES),
                                     ACT.Copy, scale=SCALE).then_inc(s_khi, 1)
                if g == 3:
                    act.wait_ge(s_wq, 16)
                    nc.scalar.activation(wq_hi[:], wq_raw[:], ACT.Copy).then_inc(s_wsplit_hi, 1)

            def copy_values(units):
                for n in units:
                    keys, c0, c1 = V_UNITS[n]
                    act.wait_ge(s_vp, n + 1)
                    src = v_bank(n)[:, 0:c1 - c0]
                    if keys in ("ip", "rest"):
                        dst = v_rest_ip if keys == "ip" else v_rest
                        nc.scalar.activation(dst[:, c0:c1], src[0:dst.shape[0], :], ACT.Copy).then_inc(s_vc, 1)
                    else:
                        b = 0 if keys == "batch 0" else 1
                        nc.scalar.activation(v_main[b][:, c0 // DH:c1 // DH, 0:DH], src.rearrange("p (h d) -> p h d", d=DH),
                                             ACT.Copy).then_inc(s_vc, 1)

            def x_high(u, count, ps):
                c0, c1 = X_CHUNKS[u]
                act.wait_ge(xt_ready, count)
                nc.scalar.activation(xt_hi[:, c0:c1, :].rearrange("p c q -> p (c q)"), ps[:, 0:(c1 - c0) * QB], ACT.Copy
                                     ).then_inc(xh_done, 1)

            for u in range(NX):
                x_high(u, u + 1, general[u % 2])

            def body(it):
                t = it.t
                if not it.back:
                    act.wait_ge(s_fill, 1 + BATCHES)
                    act.wait_ge(stored, 16 * BATCHES)
                    act.wait_ge(s_rows, 16 * BATCHES)
                for stage, kind, args, gen, sc in it.steps():
                    bank_a = general[(it.parity + gen) % 2]
                    if not it.back:
                        copy_values(V_PLACES.get((kind, *args), ()))
                        if (kind, *args) == W_O_PLACE:
                            act.wait_ge(s_wo, 16)
                            nc.scalar.activation(wo_hi, wo_raw[:, KC:2 * KC, :], ACT.Copy).then_inc(s_wsplit_hi, 1)
                    if kind == "X":
                        if args[0] == 0:
                            act.wait_ge(q_ready, t * GROUPS + GROUPS)
                        x_high(args[0], t * NX + NX + args[0] + 1, bank_a)
                    if kind == "Q":
                        g = args[0]
                        n = 0 if g in SET_A else 1
                        act.wait_ge(q_ready, t * GROUPS + g + 1)
                        if it.back:
                            act.wait_ge(stack_in[n], t * (16 * N_STACK_DMAS))
                        nc.scalar.activation(q_hi[:, g, :], bank_a[:, 0:QB], ACT.Copy).then_inc(qh_done, 1)
                    if kind == "ST":
                        g, u = args
                        act.wait_ge(st_ready, t * 15 - 15 + 3 * g + u + 1)
                        src = scores_t[(3 * g + u) % 2]
                        if u < 2:
                            if g > 0:
                                act.wait_ge(p_split, t * 10 - 10 + 2 * g + u - 1)
                            nc.scalar.activation(p_whole[:, u, :, :].rearrange("p h q -> p (h q)"), src[:], ACT.Exp)
                            nc.scalar.activation(p_hi[:, -g % P_SLOTS, 2 * u:2 * u + 2, :].rearrange("p h q -> p (h q)"), src[:],
                                                 ACT.Exp).then_inc(exp_done, 1)
                        else:
                            nc.scalar.activation(p_tail[:, -g % P_SLOTS, :], src[:, 0:QB], ACT.Exp).then_inc(exp_done, 1)
                    if kind == "AT":
                        qt, u = args
                        if (qt, u) == (0, 0):
                            act.wait_ge(p_split, t * 10 + 0)
                        act.wait_ge(at_ready[u], t * 2 - 2 + qt + 1)
                        c0, c1 = AT_CHUNKS[u]
                        nc.scalar.activation(at_hi[u][:, qt, :], scores_t[u][:, 0:P * (c1 - c0)], ACT.Copy
                                             ).then_inc(ah_done[u], 1)
                if not it.back:
                    copy_values(V_PLACES[None])

            iterations(act, body)

        @block.vector
        def _(dve):
            box, xs, ys = small[0:8, 0:4], small[0:8, 8:8 + GRID_W], small[0:8, 8 + GRID_W:8 + GRID_W + GRID_H]
            gx, gy = small[0:8, 144:144 + GRID_W], small[0:8, 208:208 + GRID_H]
            dve.wait_ge(s_grid, 48)
            nc.vector.tensor_copy(pick[0:9, :], small[0:9, 128:128 + BATCHES * IP])
            nc.vector.tensor_scalar(gx, xs, box[:, 0:1], None, ALU.is_ge)
            nc.vector.tensor_scalar(gy, ys, box[:, 1:2], None, ALU.is_ge).then_inc(s_msk, 1)
            dve.wait_ge(s_msk, 1)
            nc.vector.scalar_tensor_tensor(out=gx, in0=xs, scalar=box[:, 2:3], in1=gx, op0=ALU.is_le, op1=ALU.mult)
            nc.vector.scalar_tensor_tensor(out=gy, in0=ys, scalar=box[:, 3:4], in1=gy, op0=ALU.is_le, op1=ALU.mult
                                           ).then_inc(s_msk, 1)
            for b in range(BATCHES):
                dve.wait_ge(s_ctx_tr, 2 * b + 2)
                nc.vector.tensor_copy(ctx_t[:, 4:8, b * TEXT:b * TEXT + P],
                                      bank[2 * b + 1][:].rearrange("p (c k) -> p c k", c=4)).then_inc(s_ctx_t, 1)
            dve.wait_ge(s_ctx_tr, 5)
            rest = bank[4][:, 0:CC * BATCHES * TAIL].rearrange("p (c k) -> p c k", c=CC)
            nc.vector.tensor_copy(rest_t[:], rest)
            for b in range(BATCHES):
                nc.vector.tensor_copy(ctx_t[:, :, b * TEXT + P:(b + 1) * TEXT], rest[:, :, b * REM:(b + 1) * REM])
            nc.vector.tensor_copy(ctx_t[:, :, BATCHES * TEXT:], rest[:, :, BATCHES * REM:]).then_inc(s_ctx_t, 1)
            dve.wait_ge(s_ones_row, 1)
            dve.wait_ge(s_msk, 2)
            nc.vector.tensor_tensor(inside[0:8, :].rearrange("p (y x) -> p y x", x=GRID_W),
                                    gy.unsqueeze(2).to_broadcast([8, GRID_H, GRID_W]),
                                    gx.unsqueeze(1).to_broadcast([8, GRID_H, GRID_W]), ALU.mult).then_inc(s_msk, 1)
            dve.wait_ge(s_row_raw, 16)
            nc.vector.tensor_copy(row_consts[:], row_raw[:]).then_inc(s_row_consts, 1)
            def mask_values(first, end):
                for n in range(first, end):
                    dve.wait_ge(s_cnt, n + 1)
                    if n == 4:
                        dve.wait_ge(stored, 16)
                    c = n % 4
                    nc.vector.tensor_scalar(mask[:, 512 * c:512 * (c + 1)], bank[2 + n % 3][0:IP, :], -1.0, -NEG,
                                            ALU.max, ALU.mult).then_inc(s_mval, 1)

            for g in range(GROUPS):
                ps = k_bank(g)
                dve.wait_ge(s_khi, 2 * g + 2)
                for u, (c0, c1, k0, k1) in enumerate(((0, BATCHES * TEXT, 0, TEXT),
                                                      (BATCHES * TEXT, BATCHES * CTX, TEXT, CTX))):
                    for b in range(BATCHES):
                        w = (c1 - c0) // BATCHES
                        last = nc.vector.scalar_tensor_tensor(
                            out=k_lo[:, g, b, k0:k1], in0=ps[:, c0 + b * w:c0 + (b + 1) * w], scalar=SCALE,
                            in1=k_hi[:, g, b, k0:k1].bitcast(F32), op0=ALU.mult, op1=ALU.subtract)
                    last.then_inc(s_klo, 1)
                if g in COUNTS:
                    mask_values(*COUNTS[g])
                if g == 3:
                    dve.wait_ge(s_wsplit_hi, 1)
                    nc.vector.tensor_tensor(wq_lo[:], wq_raw[:], wq_hi[:].bitcast(F32), ALU.subtract
                                            ).then_inc(s_wsplit, 1)

            def split_values(units):
                for n in units:
                    keys, c0, c1 = V_UNITS[n]
                    if keys in ("ip", "rest"):
                        continue
                    dve.wait_ge(s_vc, n + 1)
                    first, second, third = (v_main[0 if keys == "batch 0" else 1][:, c0 // DH:c1 // DH, c:c + DH]
                                            for c in (0, VW, VB))
                    left = v_left[:, 0:c1 - c0].rearrange("p (h d) -> p h d", d=DH)
                    done = V_PARTS * (n - 4)
                    if done:
                        dve.wait_ge(s_vsplit, done)
                    nc.vector.tensor_tensor(left, v_bank(n)[:, 0:c1 - c0].rearrange("p (h d) -> p h d", d=DH), first,
                                            ALU.subtract).then_inc(s_vsplit, 1)
                    dve.wait_ge(s_vsplit, done + 1)
                    nc.vector.tensor_copy(second, left).then_inc(s_vsplit, 1)
                    dve.wait_ge(s_vsplit, done + 2)
                    nc.vector.tensor_tensor(third, left, second, ALU.subtract).then_inc(s_vsplit, 1)

            def rest_of_setup():
                dve.wait_ge(s_ktail_zero, BATCHES)
                dve.wait_ge(s_rows, 16 * BATCHES)
                for b in range(BATCHES):
                    for j in range(4):
                        nc.vector.tensor_copy(k_tail[b][0:STACK, j:HEADS:4, 32 * j:32 * j + TAIL],
                                              k_stack[b][0:STACK, j:HEADS:4, P:CTX].bitcast(F32)).then_inc(s_ktail, 1)
                split_values(V_PLACES[None])

            def x_low(u, count, ps):
                c0, c1 = X_CHUNKS[u]
                dve.wait_ge(xh_done, count)
                nc.vector.tensor_tensor(xt_lo[:, c0:c1, :].rearrange("p c q -> p (c q)"), ps[:, 0:(c1 - c0) * QB],
                                        xt_hi[:, c0:c1, :].bitcast(F32).rearrange("p c q -> p (c q)"),
                                        ALU.subtract).then_inc(gen_freed, 1)

            for u in range(NX):
                x_low(u, u + 1, general[u % 2])

            def body(it):
                t = it.t
                if not it.back:
                    dve.wait_ge(s_fill, 1 + BATCHES)
                for stage, kind, args, gen, sc in it.steps(late=("ST", 2)):
                    if not it.back:
                        split_values(V_PLACES.get((kind, *args), ()))
                    bank_a = general[(it.parity + gen) % 2]
                    if kind == "X":
                        x_low(args[0], t * NX + NX + args[0] + 1, bank_a)
                    if kind == "Q":
                        g = args[0]
                        dve.wait_ge(qh_done, t * GROUPS + g + 1)
                        nc.vector.tensor_tensor(q_lo[:, g, :], bank_a[:, 0:QB], q_hi[:, g, :].bitcast(F32),
                                                ALU.subtract).then_inc(gen_freed, 1)
                    if kind == "S":
                        g, qt = args
                        for pair in range(2):
                            dve.wait_ge(s_ready, it.sc0 + sc + pair + 1)
                            src = scores[(sc + pair) % 2][:, 0:2 * CTX].rearrange("p (h k) -> p h k", h=2)
                            dst = neg_max[:, qt, g, 4 * pair:4 * pair + 4].rearrange("p (h s) -> p h s", s=2)
                            nc.vector.tensor_reduce(dst[:, :, 0], src[:, :, 0:TEXT], AX_X, ALU.max, negate=True)
                            nc.vector.tensor_reduce(dst[:, :, 1], src[:, :, TEXT:CTX], AX_X, ALU.max, negate=True
                                                    ).then_inc(s_freed, 1)
                        for n, groups in enumerate((SET_A, SET_B)):
                            if (g, qt) == (groups[-1], QT - 1):
                                c0, c1 = 8 * groups[0], 8 * (groups[-1] + 1)
                                parts = max_parts[n][:, :, 0:2 * (c1 - c0)].rearrange("p a (m e) -> p a m e", e=2)
                                whole = neg_max[:].rearrange("p a g e -> p a (g e)")[:, :, c0:c1]
                                dve.wait_ge(s_freed, it.sc0 + sc + 2)
                                nc.vector.tensor_copy(parts[:, :, :, 0], whole).then_inc(split_hi, 1)
                                dve.wait_ge(split_hi, t * 2 + (1 if n == 0 else 0))
                                nc.vector.tensor_tensor(parts[:, :, :, 1], whole, parts[:, :, :, 0].bitcast(F32),
                                                        ALU.subtract).then_inc(split_done[n], 1)
                    if kind == "AUX":
                        n = args[0]
                        dve.wait_ge(aux_ready, t * 2 - 2 + n + 1)
                        nc.vector.tensor_copy(aux_rows[n][:], bank_a[0:aux_rows[n].shape[0], 0:QB]
                                              ).then_inc(gen_freed, 1)
                    if kind == "ST" and args[1] < 2:
                        g, u = args
                        dve.wait_ge(exp_done, t * 15 - 15 + 3 * g + u + 1)
                        nc.vector.tensor_tensor(p_lo[:, -g % P_SLOTS, 2 * u:2 * u + 2, :], p_whole[:, u, :, :],
                                                p_hi[:, -g % P_SLOTS, 2 * u:2 * u + 2, :], ALU.subtract).then_inc(p_split, 1)
                    if kind == "PV":
                        g, qt = args
                        n = t * 10 - 10 + 2 * g + qt
                        dve.wait_ge(pv_ready, n + 1)
                        nc.vector.reciprocal(inv_den[:, qt, :], product_1[qt][:, :, DH]).then_inc(recip_done, 1)
                        dve.wait_ge(recip_done, n + 1)
                        if g > 0:
                            dve.wait_ge(att_done, n - 1)
                        nc.vector.tensor_tensor(o_parts[:, qt, 0:8, :], product_1[qt][:, :, 0:DH],
                                                inv_den[:, qt, :].unsqueeze(2).to_broadcast([P, 8, DH]), ALU.mult
                                                ).then_inc(norm_first, 1)
                        nc.vector.tensor_tensor(o_parts[:, qt, 8:12, :], product_2[qt],
                                                inv_den[:, qt, 0:4].unsqueeze(2).to_broadcast([P, 4, DH]), ALU.mult
                                                ).then_inc(norm_done, 1)
                    if kind == "AT":
                        qt, u = args
                        dve.wait_ge(ah_done[u], t * 2 - 2 + qt + 1)
                        c0, c1 = AT_CHUNKS[u]
                        nc.vector.tensor_tensor(at_lo[u][:, qt, :], scores_t[u][:, 0:P * (c1 - c0)],
                                                at_hi[u][:, qt, :].bitcast(F32), ALU.subtract).then_inc(al_done[u], 1)
                    if kind == "O":
                        qt, half = args
                        if (qt, half) == (0, 0):
                            dve.wait_ge(xr_ready, t + 0)
                        dve.wait_ge(o_ready, t * 4 - 4 + 2 * qt + half + 1)
                        cols = slice(HALF * half, HALF * (half + 1))
                        nc.vector.tensor_tensor(out_sb[:, qt, cols], product[half][:, 0:HALF], x_res[:, qt, cols], ALU.add
                                                ).then_inc(out_done, 1)

                if not it.back:
                    rest_of_setup()

            iterations(dve, body)

        @block.tensor
        def _(pe):
            pe.wait_ge(s_ident, 16)
            pe.wait_ge(s_ctx, 16 * 5)
            for b in range(BATCHES):
                for half in range(2):
                    for c in range(4):
                        last = nc.tensor.transpose(bank[2 * b + half][:, P * c:P * (c + 1)],
                                                   ctx_main[:, b, P * (4 * half + c):P * (4 * half + c + 1)], ident[:])
                    last.then_inc(s_ctx_tr, 1)
            n = BATCHES * TAIL
            for c in range(CC):
                last = nc.tensor.transpose(bank[4][:, n * c:n * (c + 1)], ctx_rest[0:n, P * c:P * (c + 1)], ident[0:n, 0:n])
            last.then_inc(s_ctx_tr, 1)
            pe.wait_ge(s_ctx_t, BATCHES + 1)
            pe.wait_ge(s_ctx_t_act, BATCHES)
            text, both = BATCHES * TEXT, BATCHES * CTX
            for g in range(GROUPS):
                pe.wait_ge(s_wk[g], 32)
                if g >= 3:
                    pe.wait_ge(s_klo, 2 * (g - 2))
                ps = k_bank(g)
                for c in range(CC):
                    nc.tensor.matmul(ps[:, 0:text], w_kv[:, c, P * g:P * (g + 1)], ctx_t[:, c, 0:text],
                                     start=(c == 0), stop=(c == CC - 1))
                for c in range(CC):
                    last = nc.tensor.matmul(ps[:, text:both], w_k_ip[:, c, P * g:P * (g + 1)], ctx_t[:, c, text:both],
                                            start=(c == 0), stop=(c == CC - 1))
                last.then_inc(s_kp, 1)
                for n in range(*COUNTS.get(g, (0, 0))):
                    if n == 0:
                        pe.wait_ge(s_msk, 3)
                    b, c = n // 4, n % 4
                    if n >= 3:
                        pe.wait_ge(s_mval, n - 2)
                    nc.tensor.matmul(bank[2 + n % 3][0:IP, :], pick[0:9, IP * b:IP * (b + 1)],
                                     inside[:, 512 * c:512 * (c + 1)], start=True, stop=True).then_inc(s_cnt, 1)

            def make_values(units):
                for n in units:
                    keys, c0, c1 = V_UNITS[n]
                    if n == 0:
                        pe.wait_ge(s_klo, 2 * GROUPS)
                        pe.wait_ge(s_mval, 2 * 4)
                        pe.wait_ge(s_wv_ip, 16)
                    if n == 2:
                        pe.wait_ge(s_wv, 16 * GROUPS)
                    if n >= 4:
                        pe.wait_ge(s_vc, n - 3)
                    rows = {"ip": rest_t[:, :, BATCHES * REM:], "rest": rest_t[:, :, 0:BATCHES * REM],
                            "batch 0": ctx_t[:, :, 0:P], "batch 1": ctx_t[:, :, TEXT:TEXT + P]}[keys]
                    for c in range(CC):
                        last = nc.tensor.matmul(v_bank(n)[0:rows.shape[2], 0:c1 - c0], rows[:, c, :],
                                                (w_v_ip if keys == "ip" else w_kv)[:, c, c0:c1],
                                                start=(c == 0), stop=(c == CC - 1))
                    last.then_inc(s_vp, 1)

            def transpose_x(u, ps):
                c0, c1 = X_CHUNKS[u]
                for c in range(c0, c1):
                    for qt in range(QT):
                        at = (c - c0) * QB + qt * P
                        last = nc.tensor.transpose(ps[:, at:at + P], x_in[:, qt, P * c:P * (c + 1)], ident[:])
                last.then_inc(xt_ready, 1)

            pe.wait_ge(x_loaded, 16)
            for u in range(NX):
                if u >= 2:
                    pe.wait_ge(gen_freed, u - 1)
                transpose_x(u, general[u % 2])

            def free_general(it, gen):
                pe.wait_ge(gen_freed, it.gen0 + gen - 1)

            def split_product(ps, lhs_hi, lhs_lo, rhs_hi, rhs_lo):
                terms = [(l, r, c) for c in range(KC) for l, r in ((lhs_hi, rhs_hi), (lhs_lo, rhs_hi), (lhs_hi, rhs_lo))]
                for i, (l, r, c) in enumerate(terms):
                    last = nc.tensor.matmul(ps, l(c), r(c), start=(i == 0), stop=(i == len(terms) - 1))
                return last

            def body(it):
                t = it.t
                if not it.back:
                    pe.wait_ge(s_wsplit, 1)
                if it.back and it.batch[FRONT] != it.batch[BACK]:
                    pe.wait_ge(s_vsplit, 4 * V_PARTS)
                for stage, kind, args, gen, sc in it.steps():
                    if not it.back:
                        make_values(V_PLACES.get((kind, *args), ()))
                        if (kind, *args) == ("S", 0, 0):
                            pe.wait_ge(s_kst[0], 16 * 12)
                            pe.wait_ge(s_rows, 16 * BATCHES)
                    batch = it.batch[stage]
                    bank_a = general[(it.parity + gen) % 2]
                    if kind == "X":
                        if args[0] == 0:
                            pe.wait_ge(x_loaded, t * 16 + 32)
                        free_general(it, gen)
                        transpose_x(args[0], bank_a)
                    if kind == "Q":
                        g = args[0]
                        if g == 0:
                            pe.wait_ge(gen_freed, it.gen0 + 0)
                        free_general(it, gen)
                        cols = slice(P * g, P * (g + 1))
                        split_product(bank_a[:, 0:QB],
                                      lambda c: wq_hi[:, c, cols], lambda c: wq_lo[:, c, cols],
                                      lambda c: xt_hi[:, c, :], lambda c: xt_lo[:, c, :]).then_inc(q_ready, 1)
                    if kind == "S":
                        g, qt = args
                        if qt == 0 and g in (SET_A[0], SET_B[0]):
                            n = 0 if g in SET_A else 1
                            blocks = t + 1 if stage == FRONT else t + 0
                            pe.wait_ge(stack_in[n], blocks * (16 * N_STACK_DMAS))
                        for pair in range(2):
                            if it.back or sc + pair >= 2:
                                pe.wait_ge(s_freed, it.sc0 + sc + pair - 1)
                            for i in range(2):
                                h = 4 * g + 2 * pair + i
                                last = nc.tensor.matmul(scores[(sc + pair) % 2][:, i * CTX:(i + 1) * CTX],
                                                        q_stack[0:ROW_MAX, h, P * qt:P * (qt + 1)],
                                                        k_stack[batch][0:ROW_MAX, h, :], start=True, stop=True)
                            last.then_inc(s_ready, 1)
                    if kind == "AUX":
                        n = args[0]
                        pe.wait_ge(split_done[n], t + 0)
                        free_general(it, gen)
                        for qt in range(QT):
                            last = nc.tensor.transpose(bank_a[0:max_cols[n], P * qt:P * (qt + 1)],
                                                       max_parts[n][:, qt, :].bitcast(F32), ident[:])
                        last.then_inc(aux_ready, 1)
                    if kind == "ST":
                        g, u = args
                        if u == 0 and g in (SET_A[0], SET_B[0]):
                            n = 0 if g in SET_A else 1
                            pe.wait_ge(aux_in[n], t * (16 * len((SET_A, SET_B)[n])))
                        if g or u > 1:
                            pe.wait_ge(exp_done, t * 15 - 15 + 3 * g + u - 1)
                        ps = scores_t[(3 * g + u) % 2]
                        if u < 2:
                            for i in range(2):
                                h = 4 * g + 2 * u + i
                                last = nc.tensor.matmul(ps[:, QB * i:QB * (i + 1)], k_stack[batch][0:STACK, h, 0:P],
                                                        q_stack[0:STACK, h, :], start=True, stop=True)
                        else:
                            for i in range(4):
                                h = 4 * g + i
                                last = nc.tensor.matmul(ps[:, 0:QB], k_tail[batch][0:STACK, h, :],
                                                        q_stack[0:STACK, h, :], start=(i == 0), stop=(i == 3))
                        last.then_inc(st_ready, 1)
                    if kind == "PV":
                        g, qt = args
                        if qt == 0:
                            pe.wait_ge(exp_done, t * 15 - 15 + 3 * g + 3)
                            pe.wait_ge(p_split, t * 10 - 10 + 2 * g + 2)
                        if g > 0:
                            pe.wait_ge(norm_done, t * 10 - 10 + 2 * g + qt - 1)
                        queries = slice(P * qt, P * (qt + 1))
                        nc.tensor.matmul(product_1[qt][:, 0:8, :], p_tail[:, -g % P_SLOTS, queries],
                                         v_tail[batch][:, g, :].rearrange("p (e d) -> p e d", d=VW), start=True, stop=False)
                        for j in range(4):
                            values = v_main[batch][:, 4 * g + j, :]
                            lo, hi = (p[:, -g % P_SLOTS, j, queries] for p in (p_lo, p_hi))
                            nc.tensor.matmul(product[qt][:, VB * j + VW:VB * (j + 1)], hi, values[:, VB:VALUES],
                                             start=False, stop=False)
                            nc.tensor.matmul(product[qt][:, VB * j:VB * (j + 1)], hi, values[:, 0:VB], start=False, stop=False)
                            last = nc.tensor.matmul(product[qt][:, VB * j:VB * (j + 1)], lo, values[:, 0:VB],
                                                    start=False, stop=(j == 3))
                        last.then_inc(pv_ready, 1)
                    if kind == "AT":
                        qt, u = args
                        if (qt, u) == (0, 0):
                            pe.wait_ge(exp_done, t * 15 + 0)
                        if qt > 0:
                            pe.wait_ge(al_done[u], t * 2 - 2 + qt)
                        pe.wait_ge(att_done, t * 10 - 10 + (7 if u == 0 else 9) + qt)
                        c0, c1 = AT_CHUNKS[u]
                        for c in range(c0, c1):
                            last = nc.tensor.transpose(scores_t[u][:, P * (c - c0):P * (c - c0 + 1)],
                                                       attn[:, qt, P * c:P * (c + 1)], ident[:])
                        last.then_inc(at_ready[u], 1)
                    if kind == "O":
                        qt, half = args
                        if half == 0:
                            for u in range(2):
                                pe.wait_ge(al_done[u], t * 2 - 2 + qt + 1)
                        if qt > 0:
                            pe.wait_ge(out_done, t * 4 - 4 + 2 * qt + half - 1)
                        cols = slice(HALF * half, HALF * (half + 1))

                        def chunk(parts, c):
                            return parts[0][:, qt, P * c:P * (c + 1)] if c < AT_CHUNKS[0][1] else parts[1][:, qt, :]

                        split_product(product[half][:, 0:HALF], lambda c: chunk(at_hi, c), lambda c: chunk(at_lo, c),
                                      lambda c: wo_hi[:, c, cols], lambda c: wo_lo[:, c, cols]).then_inc(o_ready, 1)

                if not it.back:
                    make_values(V_PLACES[None])
                    pe.wait_ge(s_vc, len(V_UNITS))
                    pe.wait_ge(s_vsplit, 3 * V_PARTS + 1)
                    pe.wait_ge(s_ktail, 4 * BATCHES)
                    pe.wait_ge(s_vt, 16 * 8 * BATCHES)
                    pe.wait_ge(s_wsplit, 2)

            iterations(pe, body)


_INS = ["x", "ctx_2048", "fside_Bx4x4_0", "L0_xattn_w_q", "L0_xattn_w_k", "L0_xattn_w_v",
        "L0_xattn_w_k_ip", "L0_xattn_w_v_ip", "L0_xattn_w_out", "L0_xattn_b_out"]


def shape_constants():
    grid = np.zeros((8, GRID_W + GRID_H), np.float32)
    grid[:, :GRID_W] = np.linspace(0.0, 1.0, GRID_W, dtype=np.float32)
    grid[:, GRID_W:] = np.linspace(0.0, 1.0, GRID_H, dtype=np.float32)
    rows = np.zeros((STACK - ROW_MASK, 4, CTX), np.float32)
    for r in range(IP):
        rows[r, :, TEXT + r] = 1.0
    for j in range(4):
        rows[IP + 4 * j:IP + 4 * j + 2, j, :TEXT] = 1.0
        rows[IP + 4 * j + 2:IP + 4 * j + 4, j, TEXT:] = 1.0
    ones = np.zeros((P, 8, VW), np.float32)
    for j in range(4):
        ones[32 * j:32 * j + REM, j, DH] = 1.0
        ones[32 * j + REM:32 * j + TAIL, 4 + j, DH] = 1.0
    pick = np.zeros((9, BATCHES, IP), np.float32)
    for b in range(BATCHES):
        for m in range(4):
            pick[4 * b + m, b, :DUMMIES] = -1.0
            pick[4 * b + m, b, DUMMIES + m] = 1.0
        pick[8, b, DUMMIES:] = -1.0
    return {"identity": np.eye(P, dtype=np.float32), "grid": grid, "stack_rows": rows.reshape(STACK - ROW_MASK, -1),
            "tail_ones": ones.reshape(P, -1), "mask_pick": pick.reshape(9, -1)}


def kernel(**inputs):
    import concourse.bacc as bacc
    from concourse.bass_utils import run_bass_kernel_spmd

    nc = bacc.Bacc("TRN2", target_bir_lowering=False, num_devices=1)
    arrays = {f"in_{name}": np.ascontiguousarray(inputs[name]) for name in _INS}
    arrays |= {f"const_{name}": a for name, a in shape_constants().items()}
    args = [nc.dram_tensor(name, a.shape, mybir.dt.from_np(a.dtype), kind="ExternalInput").ap()
            for name, a in arrays.items()]
    out = nc.dram_tensor("out_0", (BATCHES, SEQ, D), F32, kind="ExternalOutput").ap()
    attention_kernel(nc, *args, out)
    r = run_bass_kernel_spmd(nc, [arrays], core_ids=[0])
    return r.results[0]["out_0"]
```
